# Optimizing a Trainium2 kernel written in Bass

```python
import numpy as np
import jax
import jax.numpy as jnp

def _softmax(x, axis=-1):
    return jax.nn.softmax(x, axis=axis)

def _gelu(x):
    return jax.nn.gelu(x, approximate=True)

def _silu(x):
    return jax.nn.silu(x)

def _sigmoid(x):
    return jax.nn.sigmoid(x)

def _layernorm(x, axis=-1, eps=1e-05):
    m = jnp.mean(x, axis=axis, keepdims=True)
    v = jnp.var(x, axis=axis, keepdims=True)
    return (x - m) / jnp.sqrt(v + eps)

def _scatter_add(tgt, idx, src, axis=0):
    return tgt.at[idx].add(src)

def _segment_sum(src, seg, n):
    return jax.ops.segment_sum(src, seg, n)
kernel_name = 'mk_gnn_ffn_d1_gnn_r8_c1c99b'

def setup_inputs(seed: int=0):
    np.random.seed(seed)
    _w = jnp.asarray

    def _rec_inputs():
        import jax
        import jax.numpy as jnp
        _gk = jax.random.key(seed)
        x = -0.0003713 + 1 * jax.random.normal(jax.random.fold_in(_gk, 1), (6250, 256), jnp.float32)
        _s = jax.random.randint(jax.random.fold_in(_gk, 2), (50000,), 0, 6250, jnp.int32)
        _d = jax.random.randint(jax.random.fold_in(_gk, 3), (50000,), 0, 6250, jnp.int32)
        _loop = jnp.arange(6250, dtype=jnp.int32)
        src = jnp.concatenate([_s, _d, _loop])
        dst = jnp.concatenate([_d, _s, _loop])
        _o = jnp.argsort(dst, stable=True)
        src = src[_o]
        dst = dst[_o]
        return (x, src, dst)
    x, src, dst = _rec_inputs()

    def _L0_gnn_setup():
        import jax, jax.numpy as jnp
        import numpy as np
        N, IN_CH, HEADS, OUT_CH, E = (6250, 256, 4, 64, 100000)
        key = jax.random.key(seed)
        k1, k2, k3, k4, k5 = jax.random.split(key, 5)
        x = jax.random.normal(k1, (N, IN_CH), dtype=jnp.float32)
        edge_index = jax.random.randint(k2, (2, E), 0, N, dtype=jnp.int64)
        bw = float(np.sqrt(6.0 / (IN_CH + HEADS * OUT_CH)))
        ba = float(np.sqrt(6.0 / (HEADS + OUT_CH)))
        weight = jax.random.uniform(k3, (IN_CH, HEADS * OUT_CH), jnp.float32, -bw, bw)
        attn_l = jax.random.uniform(k4, (HEADS, OUT_CH), jnp.float32, -ba, ba)
        attn_r = jax.random.uniform(k5, (HEADS, OUT_CH), jnp.float32, -ba, ba)
        return {'x': x, 'edge_index': edge_index, 'weight': weight, 'attn_l': attn_l, 'attn_r': attn_r}
    _L0_gnn_all = _L0_gnn_setup()
    _L0_gnn_in = {k: v for k, v in _L0_gnn_all.items() if k in ('weight', 'attn_l', 'attn_r')}
    del _L0_gnn_all

    def _L0_ffn_setup():
        import jax, jax.numpy as jnp
        import numpy as np
        B, S, H, F, E, K = (8, 512, 256, 512, 16, 2)
        EPS = 1e-05
        key = jax.random.key(seed)
        ks = jax.random.split(key, 9)
        sc = 0.02
        return {'x': jax.random.normal(ks[0], (B, S, H), dtype=jnp.float32), 'gate_w': jax.random.normal(ks[1], (H, E), dtype=jnp.float32) * sc, 'gate_b': jnp.zeros((E,), dtype=jnp.float32), 'w1': jax.random.normal(ks[2], (E, H, F), dtype=jnp.float32) * sc, 'b1': jnp.zeros((E, F), dtype=jnp.float32), 'w2': jax.random.normal(ks[3], (E, F, H), dtype=jnp.float32) * sc, 'b2': jnp.zeros((E, H), dtype=jnp.float32), 'gamma': jnp.ones((H,), dtype=jnp.float32), 'beta': jnp.zeros((H,), dtype=jnp.float32)}
    _L0_ffn_all = _L0_ffn_setup()
    _L0_ffn_in = {k: v for k, v in _L0_ffn_all.items() if k in ('gate_w', 'gate_b', 'w1', 'b1', 'w2', 'b2', 'gamma', 'beta')}
    del _L0_ffn_all
    return {'x': x, 'src': src, 'dst': dst, 'L0_gnn_weight': _L0_gnn_in['weight'], 'L0_gnn_attn_l': _L0_gnn_in['attn_l'], 'L0_gnn_attn_r': _L0_gnn_in['attn_r'], 'L0_ffn_gate_w': _L0_ffn_in['gate_w'], 'L0_ffn_gate_b': _L0_ffn_in['gate_b'], 'L0_ffn_w1': _L0_ffn_in['w1'], 'L0_ffn_b1': _L0_ffn_in['b1'], 'L0_ffn_w2': _L0_ffn_in['w2'], 'L0_ffn_b2': _L0_ffn_in['b2'], 'L0_ffn_gamma': _L0_ffn_in['gamma'], 'L0_ffn_beta': _L0_ffn_in['beta']}

def reference(x, src, dst, L0_gnn_weight, L0_gnn_attn_l, L0_gnn_attn_r, L0_ffn_gate_w, L0_ffn_gate_b, L0_ffn_w1, L0_ffn_b1, L0_ffn_w2, L0_ffn_b2, L0_ffn_gamma, L0_ffn_beta):
    import jax
    import jax.numpy as jnp

    def _L0_gnn_ref(x, edge_index, weight, attn_l, attn_r):
        import jax, jax.numpy as jnp
        import numpy as np
        N, IN_CH, HEADS, OUT_CH, E = (6250, 256, 4, 64, 100000)
        heads, out_ch = attn_l.shape
        n = x.shape[0]
        xt = jnp.matmul(x, weight).reshape(-1, heads, out_ch)
        row, col = (edge_index[0], edge_index[1])
        alpha_l = jnp.einsum('ehd,hd->eh', xt[row], attn_l)
        alpha_r = jnp.einsum('ehd,hd->eh', xt[col], attn_r)
        alpha = jax.nn.softmax(jax.nn.leaky_relu(alpha_l + alpha_r, 0.01), axis=1)
        tmp = jnp.einsum('nh,nhd->nd', alpha[:n], xt[col[:n]])
        out = jnp.broadcast_to(tmp[:, None, :], (n, heads, out_ch))
        return out.reshape(n, heads * out_ch)

    def _L0_ffn_ref(x, gate_w, gate_b, w1, b1, w2, b2, gamma, beta):
        import jax, jax.numpy as jnp
        import numpy as np
        B, S, H, F, E, K = (8, 512, 256, 512, 16, 2)
        EPS = 1e-05
        gate_logits = x @ gate_w + gate_b
        topk_vals, topk_idx = jax.lax.top_k(gate_logits, K)
        topk_w = jax.nn.softmax(topk_vals, axis=-1)
        h = jax.nn.relu(jnp.einsum('bsh,ehf->bsef', x, w1) + b1)
        expert_out = jnp.einsum('bsef,efh->bseh', h, w2) + b2
        sel = jnp.take_along_axis(expert_out, topk_idx[:, :, :, None], axis=2)
        moe = jnp.sum(topk_w[..., None] * sel, axis=2)
        y = x + moe
        mu = jnp.mean(y, axis=-1, keepdims=True)
        var = jnp.var(y, axis=-1, keepdims=True)
        return (y - mu) / jnp.sqrt(var + EPS) * gamma + beta
    edge_index = jnp.stack([src, dst])
    x = x + _L0_gnn_ref(_layernorm(x, axis=-1), edge_index, L0_gnn_weight, L0_gnn_attn_l, L0_gnn_attn_r)
    x = x + _L0_ffn_ref(_layernorm(x, axis=-1)[None], L0_ffn_gate_w, L0_ffn_gate_b, L0_ffn_w1, L0_ffn_b1, L0_ffn_w2, L0_ffn_b2, L0_ffn_gamma, L0_ffn_beta)[0]
    return x

_drawn_inputs = setup_inputs


def setup_inputs(seed=0):
    import zlib

    import numpy as np

    out = dict(_drawn_inputs(seed))
    spreads = {'L0_ffn_gate_b': (0.0, 0.1),
     'L0_ffn_b1': (0.0, 0.772),
     'L0_ffn_b2': (0.0, 0.1),
     'L0_ffn_gamma': (1.0, 0.2),
     'L0_ffn_beta': (0.0, 0.1)}
    factors = {}
    for name, (base, spread) in spreads.items():
        noise = np.random.default_rng([zlib.crc32(name.encode()), seed]).standard_normal(out[name].shape)
        drawn = base * np.exp(spread * noise) if base else spread * noise
        out[name] = jnp.asarray(drawn.astype(out[name].dtype))
    for name, factor in factors.items():
        out[name] = (out[name] * factor).astype(out[name].dtype)
    return out
```

```python
from contextlib import ExitStack

import concourse.bass as bass
from concourse import mybir

F32 = mybir.dt.float32
BF16 = mybir.dt.bfloat16
I32 = mybir.dt.int32
ALU = mybir.AluOpType
ACT = mybir.ActivationFunctionType
AX_X = mybir.AxisListType.X

P = 128
N = 6250
T = -(-N // P)
NP = T * P
C = 256
KC = C // P
HEADS, DH = 4, 64
E, K, F = 16, 2, 512
FC = F // P
EPS = 1e-5
SLOPE = 0.01
XW = C + HEADS
BLOCKS = (K * N + (K * (NP - N)) + E * (P - 1)) // P
U = 4
NO_ROW = 1 << 20


class Tile:

    def __init__(self, c, i=None):
        self.c, self.i = c, i

    def __add__(self, n):
        return Tile(self.c + n, self.i)

    def __sub__(self, n):
        return Tile(self.c - n, self.i)

    def value(self, times=1, plus=0):
        c = self.c * times + plus
        return c if self.i is None else self.i * (U * times) + c

    def least(self, times=1, plus=0):
        return self.c * times + plus


def wait_tiles(eng, sem, tile, times=1, plus=0):
    if tile.i is None and tile.least(times, plus) <= 0:
        return
    assert tile.least(times, plus) > 0
    eng.wait_ge(sem, tile.value(times, plus))


def steps(eng, first, last, body):
    rounds = (last - first + 1) // U
    if rounds > 1:
        with eng.Fori(0, rounds) as i:
            for u in range(U):
                body(Tile(first + u, i))
        first += rounds * U
    for t in range(first, last + 1):
        body(Tile(t))


def pipeline(eng, first_full, last_full, end, body):
    for t in range(first_full):
        body(Tile(t))
    steps(eng, first_full, last_full, body)
    for t in range(last_full + 1, end + 1):
        body(Tile(t))


def bass_gnn_moe(nc, x, dst_src, weight, attn_l, attn_r, gate_w, gate_b, w1, b1, w2, b2, gamma, beta, out):
    ctx = ExitStack()
    with ctx:
        def sb(name, shape, dt=F32):
            return ctx.enter_context(nc.sbuf_tensor(name, shape, dt))

        def sem(name):
            return ctx.enter_context(nc.semaphore(name))

        def sems(name, n):
            return [sem(f"{name}{i}") for i in range(n)]

        z_rows = nc.dram_tensor("z_rows", (NP, C), F32, kind="Internal").ap()
        moe_rows = nc.dram_tensor("moe_rows", (K * NP, C), F32, kind="Internal").ap()
        z_tiles = z_rows.rearrange("(p j) c -> p j c", j=T)
        x_tiles = x.rearrange("(p j) c -> p j c", j=T)
        out_tiles = out.rearrange("(p j) c -> p j c", j=T)
        moe_tiles = moe_rows.rearrange("(p j k) c -> p j (k c)", j=T, k=K)
        w1_view = w1.rearrange("e (k p) f -> e p k f", p=P)

        ident = sb("ident", [P, P])
        before = sb("before", [P, P], BF16)
        ones = sb("ones", [P, P], BF16)
        iota_lo = sb("iota_lo", [P, P])
        iota_blk = sb("iota_blk", [P, BLOCKS])
        iota_e = sb("iota_e", [P, E])
        iota_e16 = sb("iota_e16", [P, E])
        row_no = sb("row_no", [P, 1])
        choice_no = sb("choice_no", [P, T * K])
        minus_half = sb("minus_half", [P, 3])
        w_gnn = sb("w_gnn", [P, KC, XW])
        w_gnn_l = sb("w_gnn_l", [P, KC, HEADS])
        wg = sb("wg", [P, KC, E])
        bg = sb("bg", [P, E])
        w2_all = sb("w2_all", [P, E, FC * C])
        b1_rows = sb("b1_rows", [E * FC, P])
        b1_cols = sb("b1_cols", [P, E * FC])
        b2_all = sb("b2_all", [P, E, C])
        gamma_all = sb("gamma_all", [P, C])
        beta_all = sb("beta_all", [P, C])
        x2_all = sb("x2_all", [P, T, C])
        logits = sb("logits", [P, T, E])
        gate = sb("gate", [P, K, T])
        src_dst = sb("src_dst", [P, T, 2], I32)
        idx = sb("idx", [P, U, 2], I32)
        x_sd = sb("x_sd", [P, U, 2, C])
        bn = sb("bn", [P, 3, 6])
        mv = sb("mv", [P, U, 3, 2])
        ve = sb("ve", [P, 2, 3])
        rs = sb("rs", [P, U, 3])
        nb = sb("nb", [P, 2, 1])
        z_sd = sb("z_sd", [P, 2, 2, C])
        zT_sd = sb("zT_sd", [P, 2, 2 * KC * P])
        x_own = sb("x_own", [P, 2, C])
        z_last = sb("z_last", [P, U, C])
        score = sb("score", [P, HEADS])
        leaky = sb("leaky", [P, HEADS])
        top = sb("top", [P, 1])
        centred = sb("centred", [P, 2, HEADS])
        prob = sb("prob", [P, 2, HEADS])
        psum_e = sb("psum_e", [P, 2, 1])
        rsum = sb("rsum", [P, 1])
        parts = sb("parts", [P, 2, C])
        agg = sb("agg", [P, DH])
        zT = sb("zT", [P, 2, KC * P])
        w1_sb = sb("w1_sb", [P, U, KC, F])
        z_in = sb("z_in", [P, U, C])
        zT_in = sb("zT_in", [P, 2, KC * P])
        hT = sb("hT", [P, 2, F])
        moe_out = sb("moe_out", [P, U, C])
        g_idx = sb("g_idx", [P, U, 1], I32)
        s_idx = sb("s_idx", [P, U, 1], I32)
        token_of = sb("token_of", [P, BLOCKS], I32)
        dest_of = sb("dest_of", [P, BLOCKS], I32)
        expert_of = sb("expert_of", [P, BLOCKS], I32)

        bank = [ctx.enter_context(nc.psum_tensor(f"bank{i}", [P, 512], F32)) for i in range(8)]

        n_te = T * E
        work = w1_sb[:].rearrange("p u k f -> p (u k f)")
        hit0 = work[:, 0 * n_te:1 * n_te].rearrange("p (t e) -> p t e", e=E)
        hit1 = work[:, 1 * n_te:2 * n_te].rearrange("p (t e) -> p t e", e=E)
        cand = work[:, 2 * n_te:3 * n_te].rearrange("p (t e) -> p t e", e=E)
        rest = work[:, 3 * n_te:4 * n_te].rearrange("p (t e) -> p t e", e=E)
        both = zT_sd[:].rearrange("p u n -> p (u n)")[:, 0:n_te].rearrange("p (t e) -> p t e", e=E)
        attn = work[:, 0:2 * C].rearrange("p (s c) -> p s c", s=2)
        attn_prod = work[:, 2 * C:(2 + KC) * C].rearrange("p (k c) -> p k c", k=KC)
        run_a = z_in[:].rearrange("p u c -> p (u c)")[:, 0:n_te].rearrange("p (t e) -> p t e", e=E)
        run_b = moe_out[:].rearrange("p u c -> p (u c)")[:, 0:n_te].rearrange("p (t e) -> p t e", e=E)
        small = hT[:].rearrange("p u f -> p (u f)")
        m0 = small[:, 0:T]
        m1 = small[:, T:2 * T]
        i0 = small[:, 2 * T:3 * T]
        i1 = small[:, 3 * T:4 * T]
        gap = small[:, 4 * T:5 * T]
        egap = small[:, 5 * T:6 * T]
        slot = small[:, 6 * T:8 * T].rearrange("p (t k) -> p t k", k=K)
        rowsum = sb("rowsum", [P, E])
        rowsum_b = sb("rowsum_b", [P, E], BF16)
        cnt_i = sb("cnt_i", [P, E], I32)
        nblk = sb("nblk", [P, E])
        cum = sb("cum", [P, 2, E])
        base = sb("base", [P, E])
        slot_i = sb("slot_i", [P, T * K], I32)
        part_i = sb("part_i", [P, 2, T * K], I32)
        part_f = sb("part_f", [P, 2, T * K])
        past = work[:, 0:BLOCKS * E].rearrange("p (b e) -> p b e", e=E)
        lo_hot = sb("lo_hot", [P, 2, P], BF16)
        blk_hot = sb("blk_hot", [P, 2, 2, BLOCKS], BF16)
        row_f = sb("row_f", [P, BLOCKS])
        code_f = sb("code_f", [P, BLOCKS])
        empty_f = sb("empty_f", [P, BLOCKS])
        dest_f = sb("dest_f", [P, BLOCKS])
        dest_g = sb("dest_g", [P, BLOCKS], I32)
        exp_f = sb("exp_f", [P, BLOCKS])
        moe_in = x_sd[:].rearrange("p u s c -> p u (s c)")
        y = z_sd[:, :, 0, :]
        yn = z_sd[:, :, 1, :]
        yg = parts
        res = moe_out

        idx_loaded = sem("idx_loaded")
        gnn_w_loaded = sem("gnn_w_loaded")
        consts_loaded = sem("consts_loaded")
        w2_loaded = sem("w2_loaded")
        const_step = sem("const_step")
        consts_made = sem("consts_made")
        fold_step = sem("fold_step")
        gnn_w_ready = sem("gnn_w_ready")
        b1_turned = sem("b1_turned")
        b1_ready = sem("b1_ready")
        idx_copied = sem("idx_copied")
        gathered = sems("gathered", U)
        own_loaded = sems("own_loaded", 2)
        bn_d = sem("bn_d")
        bn_s = sem("bn_s")
        mv_d = sem("mv_d")
        mv_s = sem("mv_s")
        bn_r = sem("bn_r")
        mv_r = sem("mv_r")
        ve_ready = sem("ve_ready")
        rs_ready = sem("rs_ready")
        nb_ready = sem("nb_ready")
        zd_ready = sem("zd_ready")
        zs_ready = sem("zs_ready")
        turned = sem("turned")
        turned_copied = sem("turned_copied")
        xt_ready = sem("xt_ready")
        score_kept = sem("score_kept")
        score_leaky = sem("score_leaky")
        score_top = sem("score_top")
        score_ready = sem("score_ready")
        prob_ready = sem("prob_ready")
        parts_ready = sem("parts_ready")
        rsum_ready = sem("rsum_ready")
        agg_ready = sem("agg_ready")
        x2_ready = sem("x2_ready")
        z_ready = sem("z_ready")
        z_stored = sems("z_stored", U)
        z_turned = sem("z_turned")
        zT_copied = sem("zT_copied")
        logits_done = sem("logits_done")
        logits_kept = sem("logits_kept")
        route = sem("route")
        gap_ready = sem("gap_ready")
        x2_normed = sem("x2_normed")
        egap_ready = sem("egap_ready")
        rowsum_ready = sem("rowsum_ready")
        counts_done = sem("counts_done")
        beta_added = sem("beta_added")
        hot_ready = sem("hot_ready")
        hot_used = sem("hot_used")
        tables_ready = sem("tables_ready")
        w1_loaded = sems("w1_loaded", U)
        g_idx_copied = sem("g_idx_copied")
        z_gathered = sems("z_gathered", U)
        z_in_turned = sem("z_in_turned")
        zT_in_ready = sem("zT_in_ready")
        hidden_done = sem("hidden_done")
        hT_ready = sem("hT_ready")
        expert_done = sem("expert_done")
        moe_ready = sem("moe_ready")
        s_idx_ready = sem("s_idx_ready")
        moe_stored = sems("moe_stored", U)
        moe_loaded = sems("moe_loaded", U)
        z_loaded = sems("z_loaded", U)
        y_half = sem("y_half")
        y_done = sem("y_done")
        y_bn = sem("y_bn")
        y_mv = sem("y_mv")
        y_ve = sem("y_ve")
        y_rs = sem("y_rs")
        yn_ready = sem("yn_ready")
        y_nb = sem("y_nb")
        yg_ready = sem("yg_ready")
        res_ready = sem("res_ready")
        out_stored = sems("out_stored", U)

        block = ctx.enter_context(nc.Block())

        def row(buffer, tile):
            if tile.i is None:
                return buffer[:, tile.c, :]
            return buffer[:, bass.ds(tile.value(), 1), :].rearrange("p o c -> p (o c)")

        def col(buffer, tile):
            return buffer[:, bass.ds(tile.value(), 1)]

        def expert(eng, tile):
            return eng.value_load(expert_of[0:1, bass.ds(tile.value(), 1)], min_val=0, max_val=E - 1)

        def has(tile, n=T):
            return tile.i is not None or 0 <= tile.c < n

        def wait_filled(eng, ring, tile, each=16, used=0):
            n = each * (tile.c // len(ring) + 1 - used)
            assert n > 0
            eng.wait_ge(ring[tile.c % len(ring)], n if tile.i is None else tile.i * (each * U // len(ring)) + n)

        def wait_apart(eng, *waits):
            values = [eng.to_reg(t.value(1, plus)) if t.i is not None else t.value(1, plus) for _, t, plus in waits]
            eng.wait_ge(consts_made, 1)
            for (sem_, _, _), value in zip(waits, values):
                eng.wait_ge(sem_, value)

        B_FULL, B_LAST, B_END = 12, T - 1, T + 9
        POWS = T + 5

        @block.sync
        def _(sp):
            sp.dma_start(src_dst[:], dst_src).then_inc(idx_loaded, 16)
            sp.dma_start(w_gnn[:, :, 0:C], weight.rearrange("(k p) n -> p k n", p=P)).then_inc(gnn_w_loaded, 16)
            for a, at in ((attn_l, 0), (attn_r, 1)):
                sp.dma_start(attn[:, at, :], a.rearrange("(o h) d -> o (h d)", o=1).to_broadcast([P, C])).then_inc(gnn_w_loaded, 16)
            sp.dma_start(wg[:], gate_w.rearrange("(k p) e -> p k e", p=P)).then_inc(consts_loaded, 16)
            sp.dma_start(bg[:], gate_b.rearrange("(o e) -> o e", o=1).to_broadcast([P, E])).then_inc(consts_loaded, 16)
            sp.dma_start(b1_rows[:], b1.rearrange("e (c f) -> (e c) f", f=P)).then_inc(consts_loaded, 16)
            sp.dma_start(gamma_all[:], gamma.rearrange("(o c) -> o c", o=1).to_broadcast([P, C])).then_inc(consts_loaded, 16)
            sp.dma_start(beta_all[:], beta.rearrange("(o c) -> o c", o=1).to_broadcast([P, C])).then_inc(consts_loaded, 16)
            sp.dma_start(b2_all[:].rearrange("p e c -> p (e c)"),
                         b2.rearrange("(o e) c -> o (e c)", o=1).to_broadcast([P, E * C])).then_inc(consts_loaded, 16)
            for e in range(E):
                sp.dma_start(w2_all[:, e, :].rearrange("p (c n) -> p c n", n=C),
                             w2[e].rearrange("(c p) n -> p c n", p=P)).then_inc(w2_loaded, 16)

            def attention(t):
                own, norm = t - 4, t - 8
                if has(own):
                    if has(own - 2):
                        wait_tiles(sp, x2_ready, own, plus=-1)
                    sp.dma_start(x_own[:, own.c % 2, :], row(x_tiles, own)).then_inc(own_loaded[own.c % 2], 16)
                if has(norm):
                    wait_tiles(sp, z_ready, norm, plus=1)
                    sp.dma_start(row(z_tiles, norm), z_last[:, norm.c % U, :]).then_inc(z_stored[norm.c % U], 16)

            pipeline(sp, B_FULL, B_LAST, B_END, attention)

            sp.wait_ge(tables_ready, 1)

            def experts(t):
                u = t.c % U
                e = expert(sp, t)
                new = w1_view[bass.ds(e, 1)].rearrange("o p k f -> p (o k) f")
                if has(t - U, BLOCKS):
                    wait_tiles(sp, hidden_done, t, plus=1 - U)
                    old = expert(sp, t - U)
                    sp.dma_start(w1_sb[:, u], new, cond=(e != old)).then_inc(w1_loaded[u], 16)
                else:
                    sp.dma_start(w1_sb[:, u], new).then_inc(w1_loaded[u], 16)

            pipeline(sp, U, BLOCKS - 1, BLOCKS - 1, experts)

            for u in range(U):
                sp.wait_ge(moe_stored[u], 16 * len(range(u, BLOCKS, U)))

            def output(t):
                load, store = t, t - 3
                if has(load):
                    if has(load - U):
                        wait_tiles(sp, y_done, load, plus=1 - U)
                    sp.dma_start(moe_in[:, load.c % U, :], row(moe_tiles, load)).then_inc(moe_loaded[load.c % U], 16)
                    sp.dma_start(z_last[:, load.c % U, :], row(z_tiles, load)).then_inc(z_loaded[load.c % U], 16)
                if has(store):
                    wait_tiles(sp, res_ready, store, plus=1)
                    sp.dma_start(row(out_tiles, store), res[:, store.c % U, :]).then_inc(out_stored[store.c % U], 16)

            pipeline(sp, U, T - 1, T + 2, output)
            for u in range(U):
                sp.wait_ge(out_stored[u], 16 * len(range(u, T, U)))

        @block.gpsimd
        def _(pool):
            made = [0]

            def link(ins):
                made[0] += 1
                ins.then_inc(const_step, 1)
                pool.wait_ge(const_step, made[0])

            link(pool.memset(ident[:], 0.0))
            link(pool.affine_select(out=ident[:], in_=ident[:], compare_op=ALU.not_equal, fill=1.0, base=0,
                                    pattern=[[-1, P]], channel_multiplier=1))
            link(pool.memset(minus_half[:], -0.5))
            link(pool.memset(ones[:], 1.0))
            link(pool.affine_select(out=before[:], in_=ones[:], compare_op=ALU.is_gt, fill=0.0, base=0,
                                    pattern=[[1, P]], channel_multiplier=-1))
            for to, pattern, base_, by_row in ((iota_lo, [1, P], 0, 0), (iota_blk, [1, BLOCKS], 0, 0), (iota_e, [1, E], 0, 0),
                                               (iota_e16, [1, E], -E, 0), (row_no, [0, 1], 0, 1),
                                               (choice_no, [1, T * K], 1, 0)):
                link(pool.iota(to[:], [pattern], base=base_, channel_multiplier=by_row,
                               allow_small_or_imprecise_dtypes=True))
            pool.engine_nop().then_inc(consts_made, 1)
            pool.wait_ge(idx_loaded, 16)

            def attention(t):
                if has(t):
                    u = t.c % U
                    if has(t - U):
                        wait_tiles(pool, zd_ready, t, plus=1 - U)
                        wait_tiles(pool, zs_ready, t, plus=1 - U)
                    pool.tensor_copy(idx[:, u, :], row(src_dst, t)).then_inc(idx_copied, 1)
                    wait_apart(pool, (idx_copied, t, 1))
                    for s in range(2):
                        pool.indirect_dma_start(
                            x_sd[:, u, s, :], None, x, bass.IndirectOffsetOnAxis(ap=idx[:, u, s:s + 1], axis=0),
                            bounds_check=NP - 1).then_inc(gathered[u], 16)
                p = t - 2
                if has(p, POWS):
                    wait_tiles(pool, ve_ready, p, plus=1)
                    pool.tensor_tensor(rs[:, p.c % U, :], ve[:, p.c % 2, :], minus_half[:], ALU.pow).then_inc(rs_ready, 1)

            pipeline(pool, B_FULL, B_LAST, B_END, attention)

            def add_beta(t):
                wait_tiles(pool, x2_ready, t, plus=1)
                pool.tensor_tensor(row(x2_all, t), row(x2_all, t), beta_all[:], ALU.add).then_inc(beta_added, 1)

            pool.wait_ge(x2_normed, 1)
            pool.wait_ge(consts_loaded, 96)
            steps(pool, 0, T - 1, add_beta)

            pool.wait_ge(tables_ready, 1)
            for u in range(U):
                pool.wait_ge(z_stored[u], 16 * len(range(u, T, U)))

            def exchange(t):
                if has(t, BLOCKS):
                    u = t.c % U
                    if has(t - U, BLOCKS):
                        wait_tiles(pool, z_in_turned, t, plus=1 - U)
                    pool.tensor_copy(g_idx[:, u, :], col(token_of, t)).then_inc(g_idx_copied, 1)
                    wait_apart(pool, (g_idx_copied, t, 1))
                    pool.indirect_dma_start(
                        z_in[:, u, :], None, z_rows, bass.IndirectOffsetOnAxis(ap=g_idx[:, u, :], axis=0),
                        bounds_check=NP - 1).then_inc(z_gathered[u], 16)
                s = t - 4
                if has(s, BLOCKS):
                    v = s.c % U
                    wait_apart(pool, (s_idx_ready, s, 1), (moe_ready, s, 1))
                    pool.indirect_dma_start(
                        moe_rows, bass.IndirectOffsetOnAxis(ap=s_idx[:, v, :], axis=0), moe_out[:, v, :], None,
                        bounds_check=K * NP - 1, oob_is_err=False).then_inc(moe_stored[v], 16)

            pipeline(pool, 4, BLOCKS - 1, BLOCKS + 3, exchange)

            def output(t):
                a, b = t, t - 2
                if has(a):
                    wait_tiles(pool, y_ve, a, plus=1)
                    pool.tensor_tensor(rs[:, a.c % U, 0:1], ve[:, a.c % 2, 0:1], minus_half[:, 0:1], ALU.pow).then_inc(y_rs, 1)
                if has(b):
                    wait_tiles(pool, yg_ready, b, plus=1)
                    if has(b - U):
                        wait_filled(pool, out_stored, b, used=1)
                    pool.tensor_tensor(res[:, b.c % U, :], yg[:, b.c % 2, :], row(x2_all, b), ALU.add).then_inc(res_ready, 1)

            pipeline(pool, 6, T - 1, T + 1, output)

        @block.tensor
        def _(pe):
            pe.wait_ge(consts_made, 1)
            pe.wait_ge(gnn_w_ready, 1)
            pe.wait_ge(consts_loaded, 96)
            pe.transpose(bank[7][:, 0:E * FC], b1_rows[:], ident[0:E * FC, 0:E * FC]).then_inc(b1_turned, 1)

            def attention(t):
                xt, lg, tr, tz = t - 4, t - 9, t - 3, t - 8
                if has(xt):
                    wait_tiles(pe, turned_copied, xt, plus=1)
                    if has(xt - 2):
                        wait_tiles(pe, parts_ready, xt, plus=-1)
                        wait_tiles(pe, score_kept, xt, plus=-1)
                    u = xt.c % 2
                    for k in range(KC):
                        pe.matmul(bank[2 + u][:, 0:XW], zT_sd[:, u, k * P:(k + 1) * P], w_gnn[:, k, :],
                                  start=(k == 0), stop=False)
                    for k in range(KC):
                        mm = pe.matmul(bank[2 + u][:, C:XW], zT_sd[:, u, (KC + k) * P:(KC + k + 1) * P],
                                       w_gnn_l[:, k, :], start=False, stop=(k == KC - 1))
                    mm.then_inc(xt_ready, 1)
                if has(lg):
                    wait_tiles(pe, zT_copied, lg, plus=1)
                    u = lg.c % 2
                    for k in range(KC):
                        mm = pe.matmul(bank[4 + u][:, C:C + E], zT[:, u, k * P:(k + 1) * P], wg[:, k, :],
                                       start=(k == 0), stop=(k == KC - 1))
                    mm.then_inc(logits_done, 1)
                if has(tr):
                    wait_tiles(pe, zd_ready, tr, plus=1)
                    wait_tiles(pe, zs_ready, tr, plus=1)
                    if has(tr - 2):
                        wait_tiles(pe, turned_copied, tr, plus=-1)
                    u = tr.c % 2
                    for s in range(2):
                        for k in range(KC):
                            q = (s * KC + k) * P
                            mm = pe.transpose(bank[u][:, q:q + P], z_sd[:, u, s, k * P:(k + 1) * P], ident[:])
                    mm.then_inc(turned, 1)
                if has(tz):
                    wait_tiles(pe, z_ready, tz, plus=1)
                    if has(tz - 2):
                        wait_tiles(pe, logits_kept, tz, plus=-1)
                        wait_tiles(pe, zT_copied, tz, plus=-1)
                    u = tz.c % 2
                    for k in range(KC):
                        mm = pe.transpose(bank[4 + u][:, k * P:(k + 1) * P], z_last[:, tz.c % U, k * P:(k + 1) * P], ident[:])
                    mm.then_inc(z_turned, 1)

            pipeline(pe, B_FULL, B_LAST, B_END, attention)

            pe.wait_ge(rowsum_ready, 1)
            pe.matmul(bank[7][:, 0:E], before[:], rowsum_b[:], start=True, stop=True)
            pe.matmul(bank[7][:, E:2 * E], ones[:], rowsum_b[:], start=True, stop=True).then_inc(counts_done, 1)

            def tables(c):
                wait_tiles(pe, hot_ready, c, plus=1)
                first, last = c.i is None and c.c == 0, c.i is None and c.c == T * K - 1
                pe.matmul(bank[6][:, 0:2 * BLOCKS], lo_hot[:, c.c % 2, :],
                          blk_hot[:, c.c % 2, :, :].rearrange("p a b -> p (a b)"), start=first, stop=last).then_inc(hot_used, 1)

            pipeline(pe, 1, T * K - 2, T * K - 1, tables)

            def turn(t):
                u = t.c % 2
                wait_filled(pe, z_gathered, t)
                if has(t - 2, BLOCKS):
                    wait_tiles(pe, zT_in_ready, t, plus=-1)
                for k in range(KC):
                    mm = pe.transpose(bank[u][:, k * P:(k + 1) * P], z_in[:, t.c % U, k * P:(k + 1) * P], ident[:])
                mm.then_inc(z_in_turned, 1)

            def hidden(t):
                u = t.c % 2
                wait_tiles(pe, zT_in_ready, t, plus=1)
                wait_filled(pe, w1_loaded, t)
                if has(t - 2, BLOCKS):
                    wait_tiles(pe, hT_ready, t, plus=-1)
                for f in range(FC):
                    for k in range(KC):
                        mm = pe.matmul(bank[2 + u][:, f * P:(f + 1) * P], w1_sb[:, t.c % U, k, f * P:(f + 1) * P],
                                       zT_in[:, u, k * P:(k + 1) * P], start=(k == 0), stop=(k == KC - 1))
                mm.then_inc(hidden_done, 1)

            def second(t):
                u = t.c % 2
                e = expert(pe, t)
                wait_tiles(pe, hT_ready, t, plus=1)
                if has(t - 2, BLOCKS):
                    wait_tiles(pe, moe_ready, t, plus=-1)
                for f in range(FC):
                    mm = pe.matmul(bank[4 + u][:, 0:C], hT[:, u, f * P:(f + 1) * P],
                                   w2_all[:, bass.ds(e, 1), f * C:(f + 1) * C].rearrange("p o c -> p (o c)"),
                                   start=(f == 0), stop=(f == FC - 1))
                mm.then_inc(expert_done, 1)

            turn(Tile(0))
            pe.wait_ge(w2_loaded, 16 * E)

            def experts(t):
                hidden(t)
                if has(t + 1, BLOCKS):
                    turn(t + 1)
                if has(t - 1, BLOCKS):
                    second(t - 1)

            pipeline(pe, 4, BLOCKS - 2, BLOCKS - 1, experts)
            second(Tile(BLOCKS - 1))

        @block.scalar
        def _(act):
            act.wait_ge(b1_turned, 1)
            act.copy(b1_cols[:], bank[7][:, 0:E * FC]).then_inc(b1_ready, 1)

            def attention(t):
                cp, zs, cz, sm = t - 4, t - 3, t - 9, t - 5
                if has(cp):
                    wait_tiles(act, turned, cp, plus=1)
                    if has(cp - 2):
                        wait_tiles(act, xt_ready, cp, plus=-1)
                    act.copy(zT_sd[:, cp.c % 2, :], bank[cp.c % 2][:, :]).then_inc(turned_copied, 1)
                if has(cz):
                    wait_tiles(act, z_turned, cz, plus=1)
                    if has(cz - 2):
                        wait_tiles(act, logits_done, cz, plus=-1)
                    act.copy(zT[:, cz.c % 2, :], bank[4 + cz.c % 2][:, 0:C]).then_inc(zT_copied, 1)
                if has(sm):
                    u = sm.c % 2
                    wait_tiles(act, score_ready, sm, plus=1)
                    if has(sm - 2):
                        wait_tiles(act, agg_ready, sm, plus=-1)
                        wait_tiles(act, rsum_ready, sm, plus=-1)
                    act.activation(prob[:, u, :], centred[:, u, :], ACT.Exp, accum_out=psum_e[:, u, :]).then_inc(prob_ready, 1)
                    wait_tiles(act, prob_ready, sm, plus=1)
                    for h in range(HEADS):
                        a = act.activation(parts[:, u, h * DH:(h + 1) * DH], bank[2 + u][:, h * DH:(h + 1) * DH],
                                           ACT.Copy, scale=prob[:, u, h:h + 1])
                    a.then_inc(parts_ready, 1)
                if has(zs):
                    wait_tiles(act, nb_ready, zs, plus=1)
                    wait_tiles(act, rs_ready, zs, plus=1)
                    if has(zs - 2):
                        wait_tiles(act, turned, zs, plus=-1)
                    act.activation(z_sd[:, zs.c % 2, 1, :], x_sd[:, zs.c % U, 1, :], ACT.Identity,
                                   bias=nb[:, zs.c % 2, :], scale=rs[:, zs.c % U, 1:2]).then_inc(zs_ready, 1)

            pipeline(act, B_FULL, B_LAST, B_END, attention)

            act.wait_ge(gap_ready, 1)
            act.activation(egap, gap, ACT.Exp).then_inc(egap_ready, 1)
            act.wait_ge(b1_ready, 1)
            act.wait_ge(tables_ready, 1)

            def experts(t):
                u = t.c % 2
                e = expert(act, t)
                wait_tiles(act, hidden_done, t, plus=1)
                if has(t - 2, BLOCKS):
                    wait_tiles(act, expert_done, t, plus=-1)
                for f in range(FC):
                    a = act.activation(hT[:, u, f * P:(f + 1) * P], bank[2 + u][:, f * P:(f + 1) * P], ACT.Relu,
                                       bias=b1_cols[:, bass.ds(e * FC + f, 1)])
                a.then_inc(hT_ready, 1)

            pipeline(act, 4, BLOCKS - 1, BLOCKS - 1, experts)

            def output(t):
                a = t - 1
                if has(a):
                    wait_tiles(act, y_nb, a, plus=1)
                    if has(a - 2):
                        wait_tiles(act, yg_ready, a, plus=-1)
                    act.activation(yn[:, a.c % 2, :], y[:, a.c % 2, :], ACT.Identity, bias=nb[:, a.c % 2, :],
                                   scale=rs[:, a.c % U, 0:1]).then_inc(yn_ready, 1)

            pipeline(act, 4, T - 1, T, output)

        @block.vector
        def _(dve):
            dve.wait_ge(gnn_w_loaded, 48)
            folded = 0
            for s, dest in ((0, w_gnn_l[:, :, :]), (1, w_gnn[:, :, C:XW])):
                for k in range(KC):
                    ins = dve.tensor_tensor(attn_prod[:, k, :], w_gnn[:, k, 0:C], attn[:, s, :], ALU.mult)
                ins.then_inc(fold_step, 1)
                folded += 1
                dve.wait_ge(fold_step, folded)
                dve.tensor_reduce(dest, attn_prod.rearrange("p k (h d) -> p k h d", d=DH), AX_X, ALU.add).then_inc(fold_step, 1)
                folded += 1
                dve.wait_ge(fold_step, folded)
            dve.memset(mv[:], 1.0).then_inc(fold_step, 1)
            dve.wait_ge(fold_step, folded + 1)
            dve.tensor_copy(rowsum[:, 0:1], mv[:, 0, 0, 0:1]).then_inc(gnn_w_ready, 1)
            dve.wait_ge(consts_loaded, 96)

            def attention(t):
                st, nm, sc, rd, n2, lg = t - 2, t - 3, t - 5, t - 6, t - 8, t - 10
                if has(st):
                    wait_filled(dve, gathered, st, each=32)
                    dve.bn_stats(bn[:, 0, :], x_sd[:, st.c % U, 0, :]).then_inc(bn_d, 1)
                if has(sc):
                    u = sc.c % 2
                    wait_tiles(dve, xt_ready, sc, plus=1)
                    dve.tensor_copy(score[:], bank[2 + u][:, C:XW]).then_inc(score_kept, 1)
                if has(st):
                    dve.bn_stats(bn[:, 1, :], x_sd[:, st.c % U, 1, :]).then_inc(bn_s, 1)
                if has(sc):
                    wait_tiles(dve, score_kept, sc, plus=1)
                    dve.scalar_tensor_tensor(out=leaky[:], in0=score[:], scalar=SLOPE, in1=score[:], op0=ALU.mult,
                                             op1=ALU.max).then_inc(score_leaky, 1)
                if has(st):
                    wait_apart(dve, (bn_d, st, 1))
                    dve.bn_aggr(mv[:, st.c % U, 0, :], bn[:, 0, :]).then_inc(mv_d, 1)
                if has(sc):
                    wait_tiles(dve, score_leaky, sc, plus=1)
                    dve.tensor_reduce(top[:], leaky[:], AX_X, ALU.max).then_inc(score_top, 1)
                if has(st):
                    wait_apart(dve, (bn_s, st, 1))
                    dve.bn_aggr(mv[:, st.c % U, 1, :], bn[:, 1, :]).then_inc(mv_s, 1)
                if has(sc):
                    wait_tiles(dve, score_top, sc, plus=1)
                    if has(sc - 2):
                        wait_tiles(dve, prob_ready, sc, plus=-1)
                    dve.tensor_scalar(centred[:, u, :], leaky[:], top[:], None, ALU.subtract).then_inc(score_ready, 1)
                if has(rd):
                    v = rd.c % 2
                    wait_tiles(dve, parts_ready, rd, plus=1)
                    dve.reciprocal(rsum[:], psum_e[:, v, :]).then_inc(rsum_ready, 1)
                    dve.tensor_reduce(agg[:], parts[:, v, :].rearrange("p (h d) -> p d h", h=HEADS), AX_X,
                                      ALU.add).then_inc(agg_ready, 1)
                if has(st, POWS):
                    if has(st):
                        wait_tiles(dve, mv_d, st, plus=1)
                        wait_tiles(dve, mv_s, st, plus=1)
                    if has(st - 5):
                        wait_tiles(dve, mv_r, st, plus=-4)
                    if has(st - 2, POWS):
                        wait_tiles(dve, rs_ready, st, plus=-1)
                    dve.tensor_scalar(ve[:, st.c % 2, :], mv[:, st.c % U, :, 1], EPS, None, ALU.add).then_inc(ve_ready, 1)
                if has(nm):
                    w = nm.c % U
                    wait_tiles(dve, rs_ready, nm, plus=1)
                    if has(nm - 2):
                        wait_tiles(dve, zs_ready, nm, plus=-1)
                    dve.tensor_scalar(nb[:, nm.c % 2, :], mv[:, w, 1, 0:1], rs[:, w, 1:2], -1.0, ALU.mult,
                                      ALU.mult).then_inc(nb_ready, 1)
                    if has(nm - 2):
                        wait_tiles(dve, turned, nm, plus=-1)
                    dve.tensor_scalar(z_sd[:, nm.c % 2, 0, :], x_sd[:, w, 0, :], mv[:, w, 0, 0:1], rs[:, w, 0:1],
                                      ALU.subtract, ALU.mult).then_inc(zd_ready, 1)
                if has(rd):
                    wait_tiles(dve, rsum_ready, rd, plus=1)
                    wait_tiles(dve, agg_ready, rd, plus=1)
                    wait_filled(dve, own_loaded, rd)
                    dve.scalar_tensor_tensor(
                        out=row(x2_all, rd).rearrange("p (h d) -> p h d", h=HEADS),
                        in0=agg[:].rearrange("p (o d) -> p o d", o=1).to_broadcast([P, HEADS, DH]), scalar=rsum[:],
                        in1=x_own[:, v, :].rearrange("p (h d) -> p h d", h=HEADS), op0=ALU.mult,
                        op1=ALU.add).then_inc(x2_ready, 1)
                if has(lg):
                    wait_tiles(dve, logits_done, lg, plus=1)
                    dve.tensor_tensor(row(logits, lg), bank[4 + lg.c % 2][:, C:C + E], bg[:], ALU.add).then_inc(logits_kept, 1)
                if has(n2):
                    w = (n2.c + 5) % U
                    wait_tiles(dve, rs_ready, n2, plus=6)
                    if has(n2 - U):
                        wait_filled(dve, z_stored, n2, used=1)
                        wait_tiles(dve, z_turned, n2, plus=1 - U)
                    dve.tensor_scalar(z_last[:, n2.c % U, :], row(x2_all, n2), mv[:, w, 2, 0:1], rs[:, w, 2:3],
                                      ALU.subtract, ALU.mult).then_inc(z_ready, 1)
                if has(rd):
                    wait_apart(dve, (x2_ready, rd, 1))
                    dve.bn_stats(bn[:, 2, :], row(x2_all, rd)).then_inc(bn_r, 1)
                    wait_apart(dve, (bn_r, rd, 1))
                    dve.bn_aggr(mv[:, (rd.c + 5) % U, 2, :], bn[:, 2, :]).then_inc(mv_r, 1)

            pipeline(dve, B_FULL, B_LAST, B_END, attention)

            count = [0]

            def link(ins):
                count[0] += 1
                ins.then_inc(route, 1)
                dve.wait_ge(route, count[0])

            def over_e(a):
                return a.rearrange("p (t o) -> p t o", o=1).to_broadcast([P, T, E])

            def over_t(a):
                return a.rearrange("p (o e) -> p o e", o=1).to_broadcast([P, T, E])

            dve.wait_ge(logits_kept, T)
            dve.wait_ge(z_ready, T)
            dve.wait_ge(consts_made, 1)
            dve.tensor_copy(rowsum[:, 0:1], mv[:, 0, 0, 0:1]).then_inc(x2_normed, 1)

            def pick(values, largest, index, hit):
                link(dve.tensor_reduce(largest, values, AX_X, ALU.max))
                link(dve.tensor_tensor(cand, values, over_e(largest), ALU.is_equal))
                link(dve.scalar_tensor_tensor(out=cand, in0=cand, scalar=-float(E), in1=over_t(iota_e[:]),
                                              op0=ALU.mult, op1=ALU.add))
                link(dve.tensor_reduce(index, cand, AX_X, ALU.min))
                link(dve.tensor_tensor(hit, over_t(iota_e16[:]), over_e(index), ALU.is_equal))

            pick(logits[:], m0, i0, hit0)
            link(dve.scalar_tensor_tensor(out=rest, in0=hit0, scalar=-3.0e38, in1=logits[:], op0=ALU.mult, op1=ALU.add))
            pick(rest, m1, i1, hit1)
            dve.tensor_tensor(gap, m1, m0, ALU.subtract).then_inc(gap_ready, 1)
            link(dve.tensor_tensor(both, hit0, hit1, ALU.add))
            a, b, s = both, run_a, 1
            while s < T:
                dve.tensor_copy(b[:, 0:s, :], a[:, 0:s, :])
                link(dve.tensor_tensor(b[:, s:T, :], a[:, s:T, :], a[:, 0:T - s, :], ALU.add))
                a, b = b, (run_b if b is run_a else run_a)
                s *= 2
            running = a
            link(dve.tensor_copy(rowsum_b[:], running[:, T - 1, :]))
            dve.tensor_copy(rowsum[:], rowsum_b[:]).then_inc(rowsum_ready, 1)
            link(dve.tensor_tensor(rest, running, both, ALU.subtract))
            dve.wait_ge(egap_ready, 1)
            link(dve.tensor_scalar(m0, egap, 1.0, None, ALU.add))
            link(dve.reciprocal(gate[:, 0, :], m0))
            link(dve.tensor_tensor(gate[:, 1, :], egap, gate[:, 0, :], ALU.mult))
            dve.wait_ge(counts_done, 1)
            link(dve.tensor_scalar(nblk[:], bank[7][:, E:2 * E], float(P - 1), None, ALU.add))
            link(dve.tensor_copy(cnt_i[:], nblk[:]))
            link(dve.tensor_scalar(cnt_i[:], cnt_i[:], P.bit_length() - 1, None, ALU.logical_shift_right))
            link(dve.tensor_copy(nblk[:], cnt_i[:]))
            a, b, s = nblk[:], cum[:, 0, :], 1
            while s < E:
                dve.tensor_copy(b[:, 0:s], a[:, 0:s])
                link(dve.tensor_tensor(b[:, s:E], a[:, s:E], a[:, 0:E - s], ALU.add))
                a, b = b, (cum[:, 1, :] if s in (1, 4) else cum[:, 0, :])
                s *= 2
            blocks_to = a
            link(dve.tensor_tensor(base[:], blocks_to, nblk[:], ALU.subtract))
            link(dve.scalar_tensor_tensor(out=base[:], in0=base[:], scalar=float(P), in1=bank[7][:, 0:E],
                                          op0=ALU.mult, op1=ALU.add))
            link(dve.tensor_tensor(rest, rest, over_t(base[:]), ALU.add))
            for k, hit in enumerate((hit0, hit1)):
                link(dve.tensor_tensor(cand, hit, rest, ALU.mult))
                link(dve.tensor_reduce(slot[:, :, k], cand, AX_X, ALU.add))
            link(dve.tensor_copy(slot_i[:], slot.rearrange("p t k -> p (t k)")))
            link(dve.tensor_scalar(part_i[:, 0, :], slot_i[:], P - 1, None, ALU.bitwise_and))
            link(dve.tensor_scalar(part_i[:, 1, :], slot_i[:], P.bit_length() - 1, None, ALU.logical_shift_right))
            link(dve.tensor_copy(part_f[:], part_i[:]))

            def hots(c):
                u = c.c % 2
                if has(c - 2, T * K):
                    wait_tiles(dve, hot_used, c, plus=-1)
                dve.tensor_scalar(lo_hot[:, u, :], iota_lo[:], col(part_f[:, 0, :], c), None, ALU.is_equal)
                dve.tensor_scalar(blk_hot[:, u, 0, :], iota_blk[:], col(part_f[:, 1, :], c), row_no[:], ALU.is_equal, ALU.mult)
                dve.tensor_scalar(blk_hot[:, u, 1, :], iota_blk[:], col(part_f[:, 1, :], c), col(choice_no, c),
                                  ALU.is_equal, ALU.mult).then_inc(hot_ready, 1)

            pipeline(dve, 2, T * K - 1, T * K - 1, hots)

            link(dve.tensor_tensor(past, blocks_to.rearrange("p (o e) -> p o e", o=1).to_broadcast([P, BLOCKS, E]),
                                   iota_blk[:].rearrange("p (b o) -> p b o", o=1).to_broadcast([P, BLOCKS, E]), ALU.is_le))
            link(dve.tensor_reduce(exp_f[:], past, AX_X, ALU.add))
            link(dve.tensor_scalar(exp_f[:], exp_f[:], float(E - 1), None, ALU.min))
            link(dve.tensor_copy(expert_of[:], exp_f[:]))
            dve.wait_ge(hot_used, T * K)
            link(dve.tensor_copy(code_f[:], bank[6][:, BLOCKS:2 * BLOCKS]))
            link(dve.scalar_tensor_tensor(out=dest_f[:], in0=bank[6][:, 0:BLOCKS], scalar=float(K * T), in1=code_f[:],
                                          op0=ALU.mult, op1=ALU.add))
            link(dve.tensor_scalar(row_f[:], dest_f[:], -1.0, 0.0, ALU.add, ALU.max))
            link(dve.tensor_copy(dest_g[:], row_f[:]))
            link(dve.tensor_scalar(token_of[:], dest_g[:], 1, None, ALU.logical_shift_right))
            link(dve.tensor_scalar(empty_f[:], code_f[:], 0.0, float(NO_ROW), ALU.is_equal, ALU.mult))
            link(dve.scalar_tensor_tensor(out=row_f[:], in0=dest_f[:], scalar=-1.0, in1=empty_f[:], op0=ALU.add, op1=ALU.add))
            dve.tensor_copy(dest_of[:], row_f[:]).then_inc(tables_ready, 1)
            dve.wait_ge(tables_ready, 1)

            def keep(t):
                wait_tiles(dve, z_in_turned, t, plus=1)
                if has(t - 2, BLOCKS):
                    wait_tiles(dve, hidden_done, t, plus=-1)
                dve.tensor_copy(zT_in[:, t.c % 2, :], bank[t.c % 2][:, 0:C]).then_inc(zT_in_ready, 1)

            def experts(t):
                if has(t, BLOCKS):
                    keep(t)
                o = t - 2
                if has(o, BLOCKS):
                    v = o.c % U
                    if has(o - U, BLOCKS):
                        wait_filled(dve, moe_stored, o, used=1)
                    dve.tensor_copy(s_idx[:, v, :], col(dest_of, o)).then_inc(s_idx_ready, 1)
                    e = expert(dve, o)
                    wait_tiles(dve, expert_done, o, plus=1)
                    dve.tensor_tensor(moe_out[:, v, :], bank[4 + o.c % 2][:, 0:C],
                                      b2_all[:, bass.ds(e, 1), :].rearrange("p o c -> p (o c)"), ALU.add).then_inc(moe_ready, 1)

            pipeline(dve, 6, BLOCKS - 1, BLOCKS + 1, experts)

            def output(t):
                a, g = t, t - 2
                if has(a):
                    u, v = a.c % U, a.c % 2
                    wait_filled(dve, moe_loaded, a)
                    wait_filled(dve, z_loaded, a)
                    if has(a - 2):
                        wait_tiles(dve, yn_ready, a, plus=-1)
                    dve.scalar_tensor_tensor(out=y[:, v, :], in0=moe_in[:, u, 0:C], scalar=col(gate[:, 0, :], a),
                                             in1=z_last[:, u, :], op0=ALU.mult, op1=ALU.add).then_inc(y_half, 1)
                if has(g):
                    wait_tiles(dve, yn_ready, g, plus=1)
                    if has(g - 2):
                        wait_tiles(dve, res_ready, g, plus=-1)
                    dve.tensor_tensor(yg[:, g.c % 2, :], yn[:, g.c % 2, :], gamma_all[:], ALU.mult).then_inc(yg_ready, 1)
                if has(a):
                    wait_tiles(dve, y_half, a, plus=1)
                    dve.scalar_tensor_tensor(out=y[:, v, :], in0=moe_in[:, u, C:2 * C], scalar=col(gate[:, 1, :], a),
                                             in1=y[:, v, :], op0=ALU.mult, op1=ALU.add).then_inc(y_done, 1)
                    wait_apart(dve, (y_done, a, 1))
                    dve.bn_stats(bn[:, 0, :], y[:, v, :]).then_inc(y_bn, 1)
                    wait_apart(dve, (y_bn, a, 1))
                    dve.bn_aggr(mv[:, u, 0, :], bn[:, 0, :]).then_inc(y_mv, 1)
                    wait_tiles(dve, y_mv, a, plus=1)
                    dve.tensor_scalar(ve[:, v, 0:1], mv[:, u, 0, 1:2], EPS, None, ALU.add).then_inc(y_ve, 1)
                m = t - 1
                if has(m):
                    wait_tiles(dve, y_rs, m, plus=1)
                    dve.tensor_scalar(nb[:, m.c % 2, :], mv[:, m.c % U, 0, 0:1], rs[:, m.c % U, 0:1], -1.0, ALU.mult,
                                      ALU.mult).then_inc(y_nb, 1)

            pipeline(dve, 6, T - 1, T + 1, output)


_INS = ["x", "dst_src", "L0_gnn_weight", "L0_gnn_attn_l", "L0_gnn_attn_r", "L0_ffn_gate_w", "L0_ffn_gate_b", "L0_ffn_w1",
        "L0_ffn_b1", "L0_ffn_w2", "L0_ffn_b2", "L0_ffn_gamma", "L0_ffn_beta"]


def kernel(**inputs):
    import numpy as _np
    import concourse.bacc as _bacc
    from concourse import mybir as _mybir
    from concourse.bass_utils import run_bass_kernel_spmd as _run

    given = dict(inputs)
    given["x"] = _np.concatenate([_np.asarray(inputs["x"]), _np.zeros((NP - N, C), _np.float32)])
    edges = _np.zeros((P, T, 2), _np.int32)
    for at, name in ((0, "dst"), (1, "src")):
        whole = _np.zeros(NP, _np.int32)
        whole[:N] = _np.asarray(inputs[name])[:N]
        edges[:, :, at] = whole.reshape(P, T)
    given["dst_src"] = edges

    nc = _bacc.Bacc("TRN2", target_bir_lowering=False, num_devices=1)
    arrays, args = {}, []
    for name in _INS:
        a = _np.ascontiguousarray(given[name])
        arrays[f"in_{name}_dram"] = a
        args.append(nc.dram_tensor(f"in_{name}_dram", a.shape, _mybir.dt.from_np(a.dtype), kind="ExternalInput").ap())
    args.append(nc.dram_tensor("out_0_dram", (NP, C), F32, kind="ExternalOutput").ap())
    bass_gnn_moe(nc, *args)
    r = _run(nc, [arrays], core_ids=[0])
    return r.results[0]["out_0_dram"][:N]
```

```python
from contextlib import ExitStack

import concourse.bass as bass
from concourse import mybir

F32 = mybir.dt.float32
BF16 = mybir.dt.bfloat16
I32 = mybir.dt.int32
ALU = mybir.AluOpType
ACT = mybir.ActivationFunctionType
AX_X = mybir.AxisListType.X

P = 128
N = 6250
T = -(-N // P)
NP = T * P
C = 256
KC = C // P
HEADS, DH = 4, 64
E, K, F = 16, 2, 512
FC = F // P
EPS = 1e-5
SLOPE = 0.01
XW = C + HEADS
BLOCKS = (K * N + (K * (NP - N)) + E * (P - 1)) // P
U = 4
G = 7
NO_ROW = 1 << 20


class Tile:

    def __init__(self, c, i=None):
        self.c, self.i = c, i

    def __add__(self, n):
        return Tile(self.c + n, self.i)

    def __sub__(self, n):
        return Tile(self.c - n, self.i)

    def value(self, times=1, plus=0):
        c = self.c * times + plus
        return c if self.i is None else self.i * (U * times) + c

    def least(self, times=1, plus=0):
        return self.c * times + plus


def wait_tiles(eng, sem, tile, times=1, plus=0):
    if tile.i is None and tile.least(times, plus) <= 0:
        return
    assert tile.least(times, plus) > 0
    eng.wait_ge(sem, tile.value(times, plus))


def steps(eng, first, last, body):
    rounds = (last - first + 1) // U
    if rounds > 1:
        with eng.Fori(0, rounds) as i:
            for u in range(U):
                body(Tile(first + u, i))
        first += rounds * U
    for t in range(first, last + 1):
        body(Tile(t))


def pipeline(eng, first_full, last_full, end, body):
    for t in range(first_full):
        body(Tile(t))
    steps(eng, first_full, last_full, body)
    for t in range(last_full + 1, end + 1):
        body(Tile(t))


def bass_gnn_moe(nc, x, dst_src, weight, attn_l, attn_r, gate_w, gate_b, w1, b1, w2, b2, gamma, beta, out):
    ctx = ExitStack()
    with ctx:
        def sb(name, shape, dt=F32):
            return ctx.enter_context(nc.sbuf_tensor(name, shape, dt))

        def sem(name):
            return ctx.enter_context(nc.semaphore(name))

        def sems(name, n):
            return [sem(f"{name}{i}") for i in range(n)]

        z_rows = nc.dram_tensor("z_rows", (NP, C), F32, kind="Internal").ap()
        moe_rows = nc.dram_tensor("moe_rows", (K * NP, C), F32, kind="Internal").ap()
        z_tiles = z_rows.rearrange("(p j) c -> p j c", j=T)
        x_tiles = x.rearrange("(p j) c -> p j c", j=T)
        out_tiles = out.rearrange("(p j) c -> p j c", j=T)
        moe_tiles = moe_rows.rearrange("(p j k) c -> p j (k c)", j=T, k=K)
        w1_view = w1.rearrange("e (k p) f -> e p k f", p=P)

        ident = sb("ident", [P, P])
        before = sb("before", [P, P], BF16)
        ones = sb("ones", [P, P], BF16)
        iota_rep = sb("iota_rep", [P, P, G], BF16)
        iota_blk = sb("iota_blk", [P, BLOCKS])
        iota_e16 = sb("iota_e16", [P, E, T], BF16)
        row_no = sb("row_no", [P, 1])
        choice_no = sb("choice_no", [P, T * K], BF16)
        minus_half = sb("minus_half", [P, 3])
        w_gnn = sb("w_gnn", [P, KC, XW])
        w_gnn_l = sb("w_gnn_l", [P, KC, HEADS])
        wg = sb("wg", [P, KC, E])
        bg = sb("bg", [P, E])
        w2_all = sb("w2_all", [P, E, FC * C])
        b1_rows = sb("b1_rows", [E * FC, P])
        b1_cols = sb("b1_cols", [P, E * FC])
        b2_all = sb("b2_all", [P, E, C])
        gamma_all = sb("gamma_all", [P, C])
        beta_all = sb("beta_all", [P, C])
        x2_all = sb("x2_all", [P, T, C])
        logits = sb("logits", [P, E, T])
        gate = sb("gate", [P, K, T])
        rs = sb("rs", [P, T + 5, 3])
        nb_z = sb("nb_z", [P, T])
        src_dst = sb("src_dst", [P, T, 2], I32)
        idx = sb("idx", [P, U, 2], I32)
        x_sd = sb("x_sd", [P, U, 2, C])
        bn = sb("bn", [P, 3, 6])
        mv = sb("mv", [P, U, 3, 2])
        ve = sb("ve", [P, 2, 3])
        nb = sb("nb", [P, 2, 2])
        z_sd = sb("z_sd", [P, 2, 2, C])
        zT_sd = sb("zT_sd", [P, 2, 2 * KC * P])
        x_own = sb("x_own", [P, 2, C])
        z_last = sb("z_last", [P, U, C])
        score = sb("score", [P, HEADS])
        leaky = sb("leaky", [P, HEADS])
        top = sb("top", [P, 1])
        centred = sb("centred", [P, 2, HEADS])
        prob = sb("prob", [P, 2, HEADS])
        psum_e = sb("psum_e", [P, 2, 1])
        rsum = sb("rsum", [P, 1])
        parts = sb("parts", [P, 2, C])
        agg = sb("agg", [P, DH])
        zT = sb("zT", [P, 2, KC * P])
        w1_sb = sb("w1_sb", [P, U, KC, F])
        z_in = sb("z_in", [P, U, C])
        zT_in = sb("zT_in", [P, 2, KC * P])
        hT = sb("hT", [P, 2, F])
        moe_out = sb("moe_out", [P, U, C])
        g_idx = sb("g_idx", [P, U, 1], I32)
        s_idx = sb("s_idx", [P, U, 1], I32)
        token_of = sb("token_of", [P, BLOCKS], I32)
        dest_of = sb("dest_of", [P, BLOCKS], I32)
        expert_of = sb("expert_of", [P, BLOCKS], I32)

        bank = [ctx.enter_context(nc.psum_tensor(f"bank{i}", [P, 512], F32)) for i in range(8)]

        n_te = T * E
        work = w1_sb[:].rearrange("p u k f -> p (u k f)")
        work_b = work.bitcast(BF16)

        def by_expert(buffer, at):
            return buffer[:, at * n_te:(at + 1) * n_te].rearrange("p (e t) -> p e t", t=T)

        hit0, hit1, equal, lowest = (by_expert(work_b, i) for i in range(4))
        product, rest = (by_expert(work, i) for i in (2, 3))
        running = by_expert(zT_sd[:].rearrange("p u n -> p (u n)"), 0)
        n_lo, n_blk = P * G, BLOCKS * G
        lo_hot = work_b[:, 0:2 * n_lo].rearrange("p (u b g) -> p u b g", u=2, g=G)
        blk_hot = work_b[:, 2 * n_lo:2 * n_lo + 6 * n_blk].rearrange("p (u s b g) -> p u s b g", u=2, s=3, g=G)
        attn = work[:, 0:2 * C].rearrange("p (s c) -> p s c", s=2)
        attn_prod = work[:, 2 * C:(2 + KC) * C].rearrange("p (k c) -> p k c", k=KC)
        small = hT[:].rearrange("p u f -> p (u f)")
        m0 = small[:, 0:T]
        m1 = small[:, T:2 * T]
        index = sb("index", [P, K, T], BF16)
        gap = small[:, 4 * T:5 * T]
        egap = small[:, 5 * T:6 * T]
        slot = small[:, 6 * T:8 * T]
        first_slot = small[:, 8 * T:8 * T + E]
        diagonal = small[0:E, 8 * T + E:8 * T + 2 * E]
        blocks_col = small[0:E, 8 * T + 2 * E:8 * T + 2 * E + 1]
        row_ends = sb("row_ends", [P, 1 + E])
        rowsum_b = sb("rowsum_b", [P, E], BF16)
        cnt_i = sb("cnt_i", [P, E], I32)
        nblk = sb("nblk", [P, E])
        zeros_e = sb("zeros_e", [P, E])
        cum = sb("cum", [P, 2, E])
        slot_i = sb("slot_i", [P, T * K], I32)
        part_i = sb("part_i", [P, 2, T * K], I32)
        part_b = sb("part_b", [P, 2, T * K], BF16)
        past = sb("past", [E, BLOCKS], BF16)
        row_f = sb("row_f", [P, BLOCKS])
        code_f = sb("code_f", [P, BLOCKS])
        empty_f = sb("empty_f", [P, BLOCKS])
        dest_f = sb("dest_f", [P, BLOCKS])
        dest_g = sb("dest_g", [P, BLOCKS], I32)
        exp_f = sb("exp_f", [P, BLOCKS])
        moe_in = x_sd[:].rearrange("p u s c -> p u (s c)")
        y = z_sd[:].rearrange("p u s c -> p (u s) c")
        yn = zT_sd[:].rearrange("p u (s c) -> p (u s) c", c=C)
        yg = parts
        y_ve_buf = sb("y_ve_buf", [P, 2, 1])
        y_rs = sb("y_rs", [P, U, 1])
        nb_y = sb("nb_y", [P, 2, 1])
        y_mv_buf = sb("y_mv_buf", [P, U, 2])
        bn_y = sb("bn_y", [P, 2, 6])
        z_own = z_last
        res = moe_out

        idx_loaded = sem("idx_loaded")
        gnn_w_loaded = sem("gnn_w_loaded")
        gate_loaded = sem("gate_loaded")
        consts_loaded = sem("consts_loaded")
        w2_loaded = sem("w2_loaded")
        const_step = sem("const_step")
        consts_made = sem("consts_made")
        iotas_made = sem("iotas_made")
        fold_step = sem("fold_step")
        gnn_w_ready = sem("gnn_w_ready")
        b1_turned = sem("b1_turned")
        b1_ready = sem("b1_ready")
        idx_copied = sem("idx_copied")
        gathered = sems("gathered", U)
        own_loaded = sems("own_loaded", 2)
        bn_d = sem("bn_d")
        bn_s = sem("bn_s")
        mv_d = sem("mv_d")
        mv_s = sem("mv_s")
        bn_r = sem("bn_r")
        mv_r = sem("mv_r")
        nb_z_ready = sem("nb_z_ready")
        ve_ready = sem("ve_ready")
        rs_ready = sem("rs_ready")
        nb_ready = sem("nb_ready")
        norm_ready = sem("norm_ready")
        turned = sem("turned")
        turned_copied = sem("turned_copied")
        xt_ready = sem("xt_ready")
        score_kept = sem("score_kept")
        score_leaky = sem("score_leaky")
        score_top = sem("score_top")
        score_ready = sem("score_ready")
        prob_ready = sem("prob_ready")
        parts_ready = sem("parts_ready")
        rsum_ready = sem("rsum_ready")
        agg_ready = sem("agg_ready")
        x2_ready = sem("x2_ready")
        z_ready = sem("z_ready")
        z_stored = sems("z_stored", U)
        z_turned = sem("z_turned")
        zT_copied = sem("zT_copied")
        logits_done = sem("logits_done")
        logits_kept = sem("logits_kept")
        route = sem("route")
        gap_ready = sem("gap_ready")
        egap_ready = sem("egap_ready")
        rowsum_ready = sem("rowsum_ready")
        counts_done = sem("counts_done")
        past_ready = sem("past_ready")
        expert_counted = sem("expert_counted")
        expert_of_ready = sem("expert_of_ready")
        equal_ready = sem("equal_ready")
        row_hot_ready = sem("row_hot_ready")
        hot_ready = sem("hot_ready")
        hot_used = sem("hot_used")
        tables_ready = sem("tables_ready")
        w1_loaded = sems("w1_loaded", U)
        g_idx_copied = sem("g_idx_copied")
        z_gathered = sems("z_gathered", U)
        z_in_turned = sem("z_in_turned")
        zT_in_ready = sem("zT_in_ready")
        hidden_done = sem("hidden_done")
        hT_ready = sem("hT_ready")
        expert_done = sem("expert_done")
        moe_ready = sem("moe_ready")
        s_idx_ready = sem("s_idx_ready")
        moe_stored = sems("moe_stored", U)
        moe_loaded = sems("moe_loaded", U)
        z_own_ready = sem("z_own_ready")
        beta_added = sem("beta_added")
        y_half = sem("y_half")
        y_done = sem("y_done")
        y_bn = sem("y_bn")
        y_mv = sem("y_mv")
        y_ve = sem("y_ve")
        y_rs_ready = sem("y_rs_ready")
        yn_ready = sem("yn_ready")
        nb_y_ready = sem("nb_y_ready")
        yg_ready = sem("yg_ready")
        res_ready = sem("res_ready")
        out_stored = sems("out_stored", U)

        block = ctx.enter_context(nc.Block())

        def row(buffer, tile):
            if tile.i is None:
                return buffer[:, tile.c, :]
            return buffer[:, bass.ds(tile.value(), 1), :].rearrange("p o c -> p (o c)")

        def col(buffer, tile):
            return buffer[:, bass.ds(tile.value(), 1)]

        def rs_row(tile, s):
            return row(rs, tile)[:, s:s + 1]

        def expert(eng, tile):
            return eng.value_load(expert_of[0:1, bass.ds(tile.value(), 1)], min_val=0, max_val=E - 1)

        def has(tile, n=T):
            return tile.i is not None or 0 <= tile.c < n

        def wait_filled(eng, ring, tile, each=16, used=0):
            n = each * (tile.c // len(ring) + 1 - used)
            assert n > 0
            eng.wait_ge(ring[tile.c % len(ring)], n if tile.i is None else tile.i * (each * U // len(ring)) + n)

        def wait_apart(eng, *waits):
            values = [eng.to_reg(t.value(1, plus)) if t.i is not None else t.value(1, plus) for _, t, plus in waits]
            eng.wait_ge(consts_made, 1)
            for (sem_, _, _), value in zip(waits, values):
                eng.wait_ge(sem_, value)

        B_FULL, B_LAST, B_END = 12, T - 1, T + 9
        POWS = T + 5
        HOTS = T * K // G

        @block.sync
        def _(sp):
            sp.dma_start(src_dst[:], dst_src).then_inc(idx_loaded, 16)
            sp.dma_start(w_gnn[:, :, 0:C], weight.rearrange("(k p) n -> p k n", p=P)).then_inc(gnn_w_loaded, 16)
            for a, at in ((attn_l, 0), (attn_r, 1)):
                sp.dma_start(attn[:, at, :], a.rearrange("(o h) d -> o (h d)", o=1).to_broadcast([P, C])).then_inc(gnn_w_loaded, 16)
            sp.dma_start(wg[:], gate_w.rearrange("(k p) e -> p k e", p=P)).then_inc(gate_loaded, 16)
            sp.dma_start(bg[:], gate_b.rearrange("(o e) -> o e", o=1).to_broadcast([P, E])).then_inc(gate_loaded, 16)

            def attention(t):
                own, norm = t - 4, t - 8
                if has(own):
                    if has(own - 2):
                        wait_tiles(sp, x2_ready, own, plus=-1)
                    sp.dma_start(x_own[:, own.c % 2, :], row(x_tiles, own)).then_inc(own_loaded[own.c % 2], 16)
                if has(norm):
                    wait_tiles(sp, z_ready, norm, plus=1)
                    sp.dma_start(row(z_tiles, norm), z_last[:, norm.c % U, :]).then_inc(z_stored[norm.c % U], 16)

            def attention_and_w2(t):
                attention(t)
                if t.c % 2:
                    e = t.i * (U // 2) + (t.c - B_FULL) // 2
                    sp.dma_start(w2_all[:, bass.ds(e, 1), :].rearrange("p o (c n) -> p (o c) n", n=C),
                                 w2[bass.ds(e, 1)].rearrange("o (c p) n -> p (o c) n", p=P)).then_inc(w2_loaded, 16)

            for t in range(B_FULL):
                attention(Tile(t))
                if t == 4:
                    sp.dma_start(b1_rows[:], b1.rearrange("e (c f) -> (e c) f", f=P)).then_inc(consts_loaded, 16)
                    sp.dma_start(gamma_all[:], gamma.rearrange("(o c) -> o c", o=1).to_broadcast([P, C])).then_inc(consts_loaded, 16)
                    sp.dma_start(beta_all[:], beta.rearrange("(o c) -> o c", o=1).to_broadcast([P, C])).then_inc(consts_loaded, 16)
                if t == 8:
                    sp.dma_start(b2_all[:].rearrange("p e c -> p (e c)"),
                                 b2.rearrange("(o e) c -> o (e c)", o=1).to_broadcast([P, E * C])).then_inc(consts_loaded, 16)
            steps(sp, B_FULL, B_FULL + 2 * E - 1, attention_and_w2)
            for t in range(B_FULL + 2 * E, B_END + 1):
                attention(Tile(t))

            sp.wait_ge(expert_of_ready, 1)
            sp.wait_ge(hot_used, HOTS)

            def experts(t):
                u = t.c % U
                e = expert(sp, t)
                new = w1_view[bass.ds(e, 1)].rearrange("o p k f -> p (o k) f")
                if has(t - U, BLOCKS):
                    wait_tiles(sp, hidden_done, t, plus=1 - U)
                    old = expert(sp, t - U)
                    sp.dma_start(w1_sb[:, u], new, cond=(e != old)).then_inc(w1_loaded[u], 16)
                else:
                    sp.dma_start(w1_sb[:, u], new).then_inc(w1_loaded[u], 16)

            pipeline(sp, U, BLOCKS - 1, BLOCKS - 1, experts)

            for u in range(U):
                sp.wait_ge(moe_stored[u], 16 * len(range(u, BLOCKS, U)))

            def output(t):
                load, store = t, t - 10
                if has(load):
                    if has(load - U):
                        wait_tiles(sp, y_done, load, plus=1 - U)
                    sp.dma_start(moe_in[:, load.c % U, :], row(moe_tiles, load)).then_inc(moe_loaded[load.c % U], 16)
                if has(store):
                    wait_tiles(sp, res_ready, store, plus=1)
                    sp.dma_start(row(out_tiles, store), res[:, store.c % U, :]).then_inc(out_stored[store.c % U], 16)

            pipeline(sp, 13, T - 1, T + 9, output)
            for u in range(U):
                sp.wait_ge(out_stored[u], 16 * len(range(u, T, U)))

        @block.gpsimd
        def _(pool):
            made = [0]

            def link(ins):
                made[0] += 1
                ins.then_inc(const_step, 1)
                pool.wait_ge(const_step, made[0])

            link(pool.memset(ident[:], 0.0))
            link(pool.affine_select(out=ident[:], in_=ident[:], compare_op=ALU.not_equal, fill=1.0, base=0,
                                    pattern=[[-1, P]], channel_multiplier=1))
            link(pool.memset(minus_half[:], -0.5))
            link(pool.memset(ones[:], 1.0))
            link(pool.affine_select(out=before[:], in_=ones[:], compare_op=ALU.is_gt, fill=0.0, base=0,
                                    pattern=[[1, P]], channel_multiplier=-1))
            pool.engine_nop().then_inc(consts_made, 1)
            pool.wait_ge(idx_loaded, 16)

            def attention(t):
                if has(t):
                    u = t.c % U
                    if has(t - U):
                        wait_tiles(pool, norm_ready, t, plus=1 - U)
                    pool.tensor_copy(idx[:, u, :], row(src_dst, t)).then_inc(idx_copied, 1)
                    wait_apart(pool, (idx_copied, t, 1))
                    for s in range(2):
                        pool.indirect_dma_start(
                            x_sd[:, u, s, :], None, x, bass.IndirectOffsetOnAxis(ap=idx[:, u, s:s + 1], axis=0),
                            bounds_check=NP - 1).then_inc(gathered[u], 16)
                p = t - 2
                if has(p, POWS):
                    wait_tiles(pool, ve_ready, p, plus=1)
                    pool.tensor_tensor(row(rs, p), ve[:, p.c % 2, :], minus_half[:], ALU.pow).then_inc(rs_ready, 1)

            pipeline(pool, B_FULL, B_LAST, B_END, attention)

            for to, pattern, base_, by_row in (
                    (iota_e16, [[1, E], [0, T]], -E, 0), (iota_blk, [[1, BLOCKS]], 0, 0), (row_no, [[0, 1]], 0, 1),
                    (iota_rep, [[1, P], [0, G]], 0, 0), (choice_no, [[1, K], [K, T]], 1, 0)):
                pool.iota(to[:], pattern, base=base_, channel_multiplier=by_row,
                          allow_small_or_imprecise_dtypes=True).then_inc(iotas_made, 1)

            pool.wait_ge(tables_ready, 1)
            for u in range(U):
                pool.wait_ge(z_stored[u], 16 * len(range(u, T, U)))

            def exchange(t):
                if has(t, BLOCKS):
                    u = t.c % U
                    if has(t - U, BLOCKS):
                        wait_tiles(pool, z_in_turned, t, plus=1 - U)
                    pool.tensor_copy(g_idx[:, u, :], col(token_of, t)).then_inc(g_idx_copied, 1)
                    wait_apart(pool, (g_idx_copied, t, 1))
                    pool.indirect_dma_start(
                        z_in[:, u, :], None, z_rows, bass.IndirectOffsetOnAxis(ap=g_idx[:, u, :], axis=0),
                        bounds_check=NP - 1).then_inc(z_gathered[u], 16)
                s = t - 4
                if has(s, BLOCKS):
                    v = s.c % U
                    wait_apart(pool, (s_idx_ready, s, 1), (moe_ready, s, 1))
                    pool.indirect_dma_start(
                        moe_rows, bass.IndirectOffsetOnAxis(ap=s_idx[:, v, :], axis=0), moe_out[:, v, :], None,
                        bounds_check=K * NP - 1, oob_is_err=False).then_inc(moe_stored[v], 16)

            pipeline(pool, 4, BLOCKS - 1, BLOCKS + 3, exchange)

            def output(t):
                p, b, s = t - 1, t, t - 5
                if has(p):
                    wait_tiles(pool, y_ve, p, plus=1)
                    if has(p - U):
                        wait_tiles(pool, yn_ready, p, plus=1 - U)
                    pool.tensor_tensor(y_rs[:, p.c % U, :], y_ve_buf[:, p.c % 2, :], minus_half[:, 0:1], ALU.pow).then_inc(y_rs_ready, 1)
                if has(b):
                    wait_tiles(pool, z_own_ready, b, plus=1)
                    pool.tensor_tensor(row(x2_all, b), row(x2_all, b), beta_all[:], ALU.add).then_inc(beta_added, 1)
                if has(s):
                    wait_tiles(pool, beta_added, s, plus=1)
                    wait_tiles(pool, yg_ready, s, plus=1)
                    if has(s - U):
                        wait_filled(pool, out_stored, s, used=1)
                    pool.tensor_tensor(res[:, s.c % U, :], yg[:, s.c % 2, :], row(x2_all, s), ALU.add).then_inc(res_ready, 1)

            pipeline(pool, 9, T - 1, T + 4, output)

        @block.tensor
        def _(pe):
            pe.wait_ge(consts_made, 1)
            pe.wait_ge(gate_loaded, 32)

            def attention(t):
                xt, lg, tr, tz = t - 4, t - 9, t - 3, t - 8
                if has(xt):
                    if t.c == 4 and t.i is None:
                        pe.wait_ge(gnn_w_ready, 1)
                    wait_tiles(pe, turned_copied, xt, plus=1)
                    if has(xt - 2):
                        wait_tiles(pe, parts_ready, xt, plus=-1)
                        wait_tiles(pe, score_kept, xt, plus=-1)
                    u = xt.c % 2
                    for k in range(KC):
                        pe.matmul(bank[2 + u][:, 0:XW], zT_sd[:, u, k * P:(k + 1) * P], w_gnn[:, k, :],
                                  start=(k == 0), stop=False)
                    for k in range(KC):
                        mm = pe.matmul(bank[2 + u][:, C:XW], zT_sd[:, u, (KC + k) * P:(KC + k + 1) * P],
                                       w_gnn_l[:, k, :], start=False, stop=(k == KC - 1))
                    mm.then_inc(xt_ready, 1)
                if has(lg):
                    wait_tiles(pe, zT_copied, lg, plus=1)
                    u = lg.c % 2
                    for k in range(KC):
                        mm = pe.matmul(bank[4 + u][:, C:C + E], zT[:, u, k * P:(k + 1) * P], wg[:, k, :],
                                       start=(k == 0), stop=(k == KC - 1))
                    mm.then_inc(logits_done, 1)
                if has(tr):
                    wait_tiles(pe, norm_ready, tr, plus=1)
                    if has(tr - 2):
                        wait_tiles(pe, turned_copied, tr, plus=-1)
                    u = tr.c % 2
                    for s in range(2):
                        for k in range(KC):
                            q = (s * KC + k) * P
                            mm = pe.transpose(bank[u][:, q:q + P], z_sd[:, u, s, k * P:(k + 1) * P], ident[:])
                    mm.then_inc(turned, 1)
                if has(tz):
                    wait_tiles(pe, z_ready, tz, plus=1)
                    if has(tz - 2):
                        wait_tiles(pe, logits_kept, tz, plus=-1)
                        wait_tiles(pe, zT_copied, tz, plus=-1)
                    u = tz.c % 2
                    for k in range(KC):
                        mm = pe.transpose(bank[4 + u][:, k * P:(k + 1) * P], z_last[:, tz.c % U, k * P:(k + 1) * P], ident[:])
                    mm.then_inc(z_turned, 1)

            pipeline(pe, B_FULL, B_LAST, B_END, attention)

            pe.wait_ge(consts_loaded, 64)
            pe.wait_ge(turned_copied, T)
            pe.transpose(bank[0][:, 0:E * FC], b1_rows[:], ident[0:E * FC, 0:E * FC]).then_inc(b1_turned, 1)

            pe.wait_ge(rowsum_ready, 1)
            pe.matmul(bank[7][:, 0:E], before[:], rowsum_b[:], start=True, stop=True)
            pe.matmul(bank[7][:, E:2 * E], ones[:], rowsum_b[:], start=True, stop=True).then_inc(counts_done, 1)

            pe.wait_ge(past_ready, 1)
            pe.matmul(bank[7][:, 2 * E:2 * E + BLOCKS], ones[0:E, :], past[:], start=True, stop=True).then_inc(expert_counted, 1)

            def tables(h):
                wait_tiles(pe, row_hot_ready, h, plus=1)
                wait_tiles(pe, hot_ready, h, plus=1)
                first, last = h.i is None and h.c == 0, h.i is None and h.c == HOTS - 1
                for g in range(G):
                    mm = pe.matmul(bank[6][:, 0:2 * BLOCKS].rearrange("p (s b) -> p s b", s=2), lo_hot[:, h.c % 2, :, g],
                                   blk_hot[:, h.c % 2, 1:3, :, g], start=(first and g == 0), stop=(last and g == G - 1))
                mm.then_inc(hot_used, 1)

            pipeline(pe, 1, HOTS - 2, HOTS - 1, tables)

            def turn(t):
                u = t.c % 2
                wait_filled(pe, z_gathered, t)
                if has(t - 2, BLOCKS):
                    wait_tiles(pe, zT_in_ready, t, plus=-1)
                for k in range(KC):
                    mm = pe.transpose(bank[u][:, k * P:(k + 1) * P], z_in[:, t.c % U, k * P:(k + 1) * P], ident[:])
                mm.then_inc(z_in_turned, 1)

            def hidden(t):
                u = t.c % 2
                wait_tiles(pe, zT_in_ready, t, plus=1)
                wait_filled(pe, w1_loaded, t)
                if has(t - 2, BLOCKS):
                    wait_tiles(pe, hT_ready, t, plus=-1)
                for f in range(FC):
                    for k in range(KC):
                        mm = pe.matmul(bank[2 + u][:, f * P:(f + 1) * P], w1_sb[:, t.c % U, k, f * P:(f + 1) * P],
                                       zT_in[:, u, k * P:(k + 1) * P], start=(k == 0), stop=(k == KC - 1))
                mm.then_inc(hidden_done, 1)

            def second(t):
                u = t.c % 2
                e = expert(pe, t)
                wait_tiles(pe, hT_ready, t, plus=1)
                if has(t - 2, BLOCKS):
                    wait_tiles(pe, moe_ready, t, plus=-1)
                for f in range(FC):
                    mm = pe.matmul(bank[4 + u][:, 0:C], hT[:, u, f * P:(f + 1) * P],
                                   w2_all[:, bass.ds(e, 1), f * C:(f + 1) * C].rearrange("p o c -> p (o c)"),
                                   start=(f == 0), stop=(f == FC - 1))
                mm.then_inc(expert_done, 1)

            turn(Tile(0))
            pe.wait_ge(w2_loaded, 16 * E)

            def experts(t):
                hidden(t)
                if has(t + 1, BLOCKS):
                    turn(t + 1)
                if has(t - 1, BLOCKS):
                    second(t - 1)

            pipeline(pe, 4, BLOCKS - 2, BLOCKS - 1, experts)
            second(Tile(BLOCKS - 1))

        @block.scalar
        def _(act):
            def attention(t):
                cp, zs, cz, sm = t - 4, t - 3, t - 9, t - 5
                if has(cp):
                    wait_tiles(act, turned, cp, plus=1)
                    if has(cp - 2):
                        wait_tiles(act, xt_ready, cp, plus=-1)
                    act.copy(zT_sd[:, cp.c % 2, :], bank[cp.c % 2][:, :]).then_inc(turned_copied, 1)
                if has(cz):
                    wait_tiles(act, z_turned, cz, plus=1)
                    if has(cz - 2):
                        wait_tiles(act, logits_done, cz, plus=-1)
                    act.copy(zT[:, cz.c % 2, :], bank[4 + cz.c % 2][:, 0:C]).then_inc(zT_copied, 1)
                if has(sm):
                    u = sm.c % 2
                    wait_tiles(act, score_ready, sm, plus=1)
                    if has(sm - 2):
                        wait_tiles(act, agg_ready, sm, plus=-1)
                        wait_tiles(act, rsum_ready, sm, plus=-1)
                    act.activation(prob[:, u, :], centred[:, u, :], ACT.Exp, accum_out=psum_e[:, u, :]).then_inc(prob_ready, 1)
                    wait_tiles(act, prob_ready, sm, plus=1)
                    for h in range(HEADS):
                        a = act.activation(parts[:, u, h * DH:(h + 1) * DH], bank[2 + u][:, h * DH:(h + 1) * DH],
                                           ACT.Copy, scale=prob[:, u, h:h + 1])
                    a.then_inc(parts_ready, 1)
                if has(zs):
                    wait_tiles(act, nb_ready, zs, plus=1)
                    wait_tiles(act, rs_ready, zs, plus=1)
                    if has(zs - 2):
                        wait_tiles(act, turned, zs, plus=-1)
                    for s in range(2):
                        a = act.activation(z_sd[:, zs.c % 2, s, :], x_sd[:, zs.c % U, s, :], ACT.Identity,
                                           bias=nb[:, zs.c % 2, s:s + 1], scale=rs_row(zs, s))
                    a.then_inc(norm_ready, 1)

            pipeline(act, B_FULL, B_LAST, B_END, attention)

            act.wait_ge(b1_turned, 1)
            act.copy(b1_cols[:], bank[0][:, 0:E * FC]).then_inc(b1_ready, 1)
            act.wait_ge(gap_ready, 1)
            act.activation(egap, gap, ACT.Exp).then_inc(egap_ready, 1)

            def row_hots(h):
                wait_tiles(act, equal_ready, h, plus=1)
                if has(h - 2, HOTS):
                    wait_tiles(act, hot_used, h, plus=-1)
                act.activation(blk_hot[:, h.c % 2, 1, :, :], blk_hot[:, h.c % 2, 0, :, :], ACT.Copy,
                               scale=row_no[:]).then_inc(row_hot_ready, 1)

            act.wait_ge(iotas_made, 5)
            pipeline(act, 2, HOTS - 1, HOTS - 1, row_hots)
            act.wait_ge(b1_ready, 1)
            act.wait_ge(expert_of_ready, 1)

            def experts(t):
                u = t.c % 2
                e = expert(act, t)
                wait_tiles(act, hidden_done, t, plus=1)
                if has(t - 2, BLOCKS):
                    wait_tiles(act, expert_done, t, plus=-1)
                for f in range(FC):
                    a = act.activation(hT[:, u, f * P:(f + 1) * P], bank[2 + u][:, f * P:(f + 1) * P], ACT.Relu,
                                       bias=b1_cols[:, bass.ds(e * FC + f, 1)])
                a.then_inc(hT_ready, 1)

            pipeline(act, 4, BLOCKS - 1, BLOCKS - 1, experts)

            def output(t):
                z, a = t + 1, t - 3
                if has(z):
                    if has(z - U):
                        wait_tiles(act, y_half, z, plus=1 - U)
                    act.activation(z_own[:, z.c % U, :], row(x2_all, z), ACT.Identity, bias=col(nb_z, z),
                                   scale=rs_row(z + 5, 2)).then_inc(z_own_ready, 1)
                if has(a):
                    wait_tiles(act, nb_y_ready, a, plus=1)
                    if has(a - U):
                        wait_tiles(act, yg_ready, a, plus=1 - U)
                    act.activation(yn[:, a.c % U, :], y[:, a.c % U, :], ACT.Identity, bias=nb_y[:, a.c % 2, :],
                                   scale=y_rs[:, a.c % U, :]).then_inc(yn_ready, 1)

            act.wait_ge(nb_z_ready, T)
            output(Tile(-1))
            pipeline(act, 8, T - 2, T + 2, output)

        @block.vector
        def _(dve):
            dve.wait_ge(gnn_w_loaded, 48)
            folded = 0
            for s, dest in ((0, w_gnn_l[:, :, :]), (1, w_gnn[:, :, C:XW])):
                for k in range(KC):
                    ins = dve.tensor_tensor(attn_prod[:, k, :], w_gnn[:, k, 0:C], attn[:, s, :], ALU.mult)
                ins.then_inc(fold_step, 1)
                folded += 1
                dve.wait_ge(fold_step, folded)
                dve.tensor_reduce(dest, attn_prod.rearrange("p k (h d) -> p k h d", d=DH), AX_X, ALU.add).then_inc(fold_step, 1)
                folded += 1
                dve.wait_ge(fold_step, folded)
            dve.memset(zeros_e[:], 0.0)
            dve.memset(mv[:], 1.0).then_inc(fold_step, 1)
            dve.wait_ge(fold_step, folded + 1)
            dve.tensor_copy(row_ends[:, 0:1], mv[:, 0, 0, 0:1]).then_inc(gnn_w_ready, 1)
            dve.wait_ge(gate_loaded, 32)

            def attention(t):
                st, nm, sc, rd, n2, lg = t - 2, t - 3, t - 5, t - 6, t - 8, t - 10
                if has(st):
                    wait_filled(dve, gathered, st, each=32)
                    dve.bn_stats(bn[:, 0, :], x_sd[:, st.c % U, 0, :]).then_inc(bn_d, 1)
                if has(rd - 1):
                    wait_apart(dve, (bn_r, rd - 1, 1))
                    dve.bn_aggr(mv[:, (rd.c + 4) % U, 2, :], bn[:, 2, :]).then_inc(mv_r, 1)
                if has(sc):
                    u = sc.c % 2
                    wait_tiles(dve, xt_ready, sc, plus=1)
                    dve.tensor_copy(score[:], bank[2 + u][:, C:XW]).then_inc(score_kept, 1)
                if has(st):
                    dve.bn_stats(bn[:, 1, :], x_sd[:, st.c % U, 1, :]).then_inc(bn_s, 1)
                if has(sc):
                    wait_tiles(dve, score_kept, sc, plus=1)
                    dve.scalar_tensor_tensor(out=leaky[:], in0=score[:], scalar=SLOPE, in1=score[:], op0=ALU.mult,
                                             op1=ALU.max).then_inc(score_leaky, 1)
                if has(st):
                    wait_apart(dve, (bn_d, st, 1))
                    dve.bn_aggr(mv[:, st.c % U, 0, :], bn[:, 0, :]).then_inc(mv_d, 1)
                if has(sc):
                    wait_tiles(dve, score_leaky, sc, plus=1)
                    dve.tensor_reduce(top[:], leaky[:], AX_X, ALU.max).then_inc(score_top, 1)
                if has(st):
                    wait_apart(dve, (bn_s, st, 1))
                    dve.bn_aggr(mv[:, st.c % U, 1, :], bn[:, 1, :]).then_inc(mv_s, 1)
                if has(sc):
                    wait_tiles(dve, score_top, sc, plus=1)
                    if has(sc - 2):
                        wait_tiles(dve, prob_ready, sc, plus=-1)
                    dve.tensor_scalar(centred[:, u, :], leaky[:], top[:], None, ALU.subtract).then_inc(score_ready, 1)
                if has(rd):
                    v = rd.c % 2
                    wait_tiles(dve, parts_ready, rd, plus=1)
                    dve.reciprocal(rsum[:], psum_e[:, v, :]).then_inc(rsum_ready, 1)
                    dve.tensor_reduce(agg[:], parts[:, v, :].rearrange("p (h d) -> p d h", h=HEADS), AX_X,
                                      ALU.add).then_inc(agg_ready, 1)
                if has(st, POWS):
                    if has(st):
                        wait_tiles(dve, mv_d, st, plus=1)
                        wait_tiles(dve, mv_s, st, plus=1)
                    if has(st - 5):
                        wait_tiles(dve, mv_r, st, plus=-4)
                    if has(st - 2, POWS):
                        wait_tiles(dve, rs_ready, st, plus=-1)
                    dve.tensor_scalar(ve[:, st.c % 2, :], mv[:, st.c % U, :, 1], EPS, None, ALU.add).then_inc(ve_ready, 1)
                if has(nm):
                    w = nm.c % U
                    wait_tiles(dve, rs_ready, nm, plus=1)
                    if has(nm - 2):
                        wait_tiles(dve, norm_ready, nm, plus=-1)
                    dve.scalar_tensor_tensor(out=nb[:, nm.c % 2, :], in0=mv[:, w, 0:2, 0], scalar=-1.0,
                                             in1=row(rs, nm)[:, 0:2], op0=ALU.mult, op1=ALU.mult).then_inc(nb_ready, 1)
                if has(rd):
                    wait_tiles(dve, rsum_ready, rd, plus=1)
                    wait_tiles(dve, agg_ready, rd, plus=1)
                    wait_filled(dve, own_loaded, rd)
                    dve.scalar_tensor_tensor(
                        out=row(x2_all, rd).rearrange("p (h d) -> p h d", h=HEADS),
                        in0=agg[:].rearrange("p (o d) -> p o d", o=1).to_broadcast([P, HEADS, DH]), scalar=rsum[:],
                        in1=x_own[:, v, :].rearrange("p (h d) -> p h d", h=HEADS), op0=ALU.mult,
                        op1=ALU.add).then_inc(x2_ready, 1)
                if has(lg):
                    wait_tiles(dve, logits_done, lg, plus=1)
                    dve.tensor_tensor(logits[:, :, bass.ds(lg.value(), 1)].rearrange("p e o -> p (e o)"), bank[4 + lg.c % 2][:, C:C + E], bg[:], ALU.add).then_inc(logits_kept, 1)
                if has(n2):
                    w = (n2.c + 5) % U
                    wait_tiles(dve, rs_ready, n2, plus=6)
                    dve.tensor_scalar(col(nb_z, n2), mv[:, w, 2, 0:1], rs_row(n2 + 5, 2), -1.0, ALU.mult,
                                      ALU.mult).then_inc(nb_z_ready, 1)
                    if has(n2 - U):
                        wait_filled(dve, z_stored, n2, used=1)
                        wait_tiles(dve, z_turned, n2, plus=1 - U)
                    dve.tensor_scalar(z_last[:, n2.c % U, :], row(x2_all, n2), mv[:, w, 2, 0:1], rs_row(n2 + 5, 2),
                                      ALU.subtract, ALU.mult).then_inc(z_ready, 1)
                if has(rd):
                    wait_apart(dve, (x2_ready, rd, 1))
                    dve.bn_stats(bn[:, 2, :], row(x2_all, rd)).then_inc(bn_r, 1)

            pipeline(dve, B_FULL, B_LAST, B_END, attention)

            count = [0]

            def link(ins):
                count[0] += 1
                ins.then_inc(route, 1)
                dve.wait_ge(route, count[0])

            def over_e(a):
                return a.rearrange("p (o t) -> p o t", o=1).to_broadcast([P, E, T])

            def over_t(a):
                return a.rearrange("p (e o) -> p e o", o=1).to_broadcast([P, E, T])

            def by_tile(a):
                return a.rearrange("p e t -> p t e")

            dve.wait_ge(logits_kept, T)
            dve.wait_ge(iotas_made, 5)

            def pick(values, largest, lowest_index, hit):
                link(dve.tensor_reduce(largest, by_tile(values), AX_X, ALU.max))
                link(dve.tensor_tensor(equal, values, over_e(largest), ALU.is_equal))
                link(dve.tensor_tensor(lowest, equal, iota_e16[:], ALU.mult))
                link(dve.tensor_reduce(lowest_index, by_tile(lowest), AX_X, ALU.min))
                link(dve.tensor_tensor(hit, iota_e16[:], over_e(lowest_index), ALU.is_equal))

            pick(logits[:], m0, index[:, 0, :], hit0)
            link(dve.scalar_tensor_tensor(out=rest, in0=hit0, scalar=-3.0e38, in1=logits[:], op0=ALU.mult, op1=ALU.add))
            pick(rest, m1, index[:, 1, :], hit1)
            dve.tensor_tensor(gap, m1, m0, ALU.subtract).then_inc(gap_ready, 1)
            dve.memset(row_ends[:, 0:1], 0.0)
            link(dve.tensor_tensor_scan(running.rearrange("p e t -> p (e t)"), hit0.rearrange("p e t -> p (e t)"),
                                        hit1.rearrange("p e t -> p (e t)"), 0.0, ALU.add, ALU.add))
            link(dve.tensor_copy(row_ends[:, 1:1 + E], running[:, :, T - 1]))
            dve.tensor_tensor(rowsum_b[:], row_ends[:, 1:1 + E], row_ends[:, 0:E], ALU.subtract).then_inc(rowsum_ready, 1)
            dve.wait_ge(egap_ready, 1)
            link(dve.tensor_scalar(m0, egap, 1.0, None, ALU.add))
            link(dve.reciprocal(gate[:, 0, :], m0))
            link(dve.tensor_tensor(gate[:, 1, :], egap, gate[:, 0, :], ALU.mult))
            dve.wait_ge(counts_done, 1)
            link(dve.tensor_scalar(nblk[:], bank[7][:, E:2 * E], float(P - 1), None, ALU.add))
            link(dve.tensor_copy(cnt_i[:], nblk[:]))
            link(dve.tensor_scalar(cnt_i[:], cnt_i[:], P.bit_length() - 1, None, ALU.logical_shift_right))
            link(dve.tensor_copy(nblk[:], cnt_i[:]))
            blocks_to = cum[:, 0, :]
            link(dve.tensor_tensor_scan(blocks_to, nblk[:], zeros_e[:], 0.0, ALU.add, ALU.add))
            link(dve.tensor_tensor(first_slot, blocks_to, nblk[:], ALU.subtract))
            link(dve.scalar_tensor_tensor(out=first_slot, in0=first_slot, scalar=float(P), in1=bank[7][:, 0:E],
                                          op0=ALU.mult, op1=ALU.add))
            link(dve.scalar_tensor_tensor(out=first_slot, in0=row_ends[:, 0:E], scalar=1.0, in1=first_slot,
                                          op0=ALU.add, op1=ALU.subtract))
            link(dve.tensor_tensor(diagonal, cum[0:E, 0, :], ident[0:E, 0:E], ALU.mult))
            link(dve.tensor_reduce(blocks_col, diagonal, AX_X, ALU.add))
            dve.tensor_scalar(past[:], iota_blk[0:E, :], blocks_col, None, ALU.is_ge).then_inc(past_ready, 1)
            link(dve.tensor_tensor(rest, running, over_t(first_slot), ALU.subtract))
            for k, hit in enumerate((hit0, hit1)):
                link(dve.tensor_tensor(product, hit, rest, ALU.mult))
                link(dve.tensor_reduce(slot[:, k * T:(k + 1) * T], by_tile(product), AX_X, ALU.add))
            link(dve.tensor_copy(slot_i[:], slot))
            dve.tensor_scalar(part_i[:, 0, :], slot_i[:], P - 1, None, ALU.bitwise_and)
            link(dve.tensor_scalar(part_i[:, 1, :], slot_i[:], P.bit_length() - 1, None, ALU.logical_shift_right))
            link(dve.tensor_copy(part_b[:], part_i[:]))
            dve.wait_ge(expert_counted, 1)
            link(dve.tensor_scalar(exp_f[:], bank[7][:, 2 * E:2 * E + BLOCKS], float(E - 1), None, ALU.min))
            dve.tensor_copy(expert_of[:], exp_f[:]).then_inc(expert_of_ready, 1)

            def group(a, h, n):
                cols = a[:, bass.ds(h.value(G), G)]
                return cols.rearrange("p (o g) -> p o g", o=1).to_broadcast([P, n, G])

            def hots(h):
                u = h.c % 2
                if has(h - 2, HOTS):
                    wait_tiles(dve, hot_used, h, plus=-1)
                dve.tensor_tensor(blk_hot[:, u, 0, :, :], iota_rep[:, 0:BLOCKS, :], group(part_b[:, 1, :], h, BLOCKS),
                                  ALU.is_equal).then_inc(equal_ready, 1)
                dve.tensor_tensor(lo_hot[:, u, :, :], iota_rep[:], group(part_b[:, 0, :], h, P), ALU.is_equal)
                wait_tiles(dve, equal_ready, h, plus=1)
                dve.tensor_tensor(blk_hot[:, u, 2, :, :], blk_hot[:, u, 0, :, :], group(choice_no, h, BLOCKS),
                                  ALU.mult).then_inc(hot_ready, 1)

            pipeline(dve, 2, HOTS - 1, HOTS - 1, hots)

            dve.wait_ge(hot_used, HOTS)
            link(dve.tensor_copy(code_f[:], bank[6][:, BLOCKS:2 * BLOCKS]))
            link(dve.scalar_tensor_tensor(out=dest_f[:], in0=bank[6][:, 0:BLOCKS], scalar=float(K * T), in1=code_f[:],
                                          op0=ALU.mult, op1=ALU.add))
            link(dve.tensor_scalar(row_f[:], dest_f[:], -1.0, 0.0, ALU.add, ALU.max))
            link(dve.tensor_copy(dest_g[:], row_f[:]))
            dve.tensor_scalar(token_of[:], dest_g[:], 1, None, ALU.logical_shift_right).then_inc(tables_ready, 1)
            link(dve.tensor_scalar(empty_f[:], code_f[:], 0.0, float(NO_ROW), ALU.is_equal, ALU.mult))
            link(dve.scalar_tensor_tensor(out=row_f[:], in0=dest_f[:], scalar=-1.0, in1=empty_f[:], op0=ALU.add, op1=ALU.add))
            link(dve.tensor_copy(dest_of[:], row_f[:]))
            dve.wait_ge(expert_of_ready, 1)
            dve.wait_ge(consts_loaded, 64)

            def keep(t):
                wait_tiles(dve, z_in_turned, t, plus=1)
                if has(t - 2, BLOCKS):
                    wait_tiles(dve, hidden_done, t, plus=-1)
                dve.tensor_copy(zT_in[:, t.c % 2, :], bank[t.c % 2][:, 0:C]).then_inc(zT_in_ready, 1)

            def experts(t):
                if has(t, BLOCKS):
                    keep(t)
                o = t - 2
                if has(o, BLOCKS):
                    v = o.c % U
                    if has(o - U, BLOCKS):
                        wait_filled(dve, moe_stored, o, used=1)
                    dve.tensor_copy(s_idx[:, v, :], col(dest_of, o)).then_inc(s_idx_ready, 1)
                    e = expert(dve, o)
                    wait_tiles(dve, expert_done, o, plus=1)
                    dve.tensor_tensor(moe_out[:, v, :], bank[4 + o.c % 2][:, 0:C],
                                      b2_all[:, bass.ds(e, 1), :].rearrange("p o c -> p (o c)"), ALU.add).then_inc(moe_ready, 1)

            pipeline(dve, 6, BLOCKS - 1, BLOCKS + 1, experts)

            def output(t):
                a, m, n, g = t, t - 1, t - 2, t - 4
                if has(a):
                    wait_filled(dve, moe_loaded, a)
                    wait_tiles(dve, z_own_ready, a, plus=1)
                    if has(a - U):
                        wait_tiles(dve, yn_ready, a, plus=1 - U)
                    dve.scalar_tensor_tensor(out=y[:, a.c % U, :], in0=moe_in[:, a.c % U, 0:C], scalar=col(gate[:, 0, :], a),
                                             in1=z_own[:, a.c % U, :], op0=ALU.mult, op1=ALU.add).then_inc(y_half, 1)
                if has(m):
                    wait_apart(dve, (y_bn, m, 1))
                    dve.bn_aggr(y_mv_buf[:, m.c % U, :], bn_y[:, m.c % 2, :]).then_inc(y_mv, 1)
                if has(a):
                    wait_tiles(dve, y_half, a, plus=1)
                    dve.scalar_tensor_tensor(out=y[:, a.c % U, :], in0=moe_in[:, a.c % U, C:2 * C],
                                             scalar=col(gate[:, 1, :], a), in1=y[:, a.c % U, :], op0=ALU.mult,
                                             op1=ALU.add).then_inc(y_done, 1)
                if has(m):
                    wait_tiles(dve, y_mv, m, plus=1)
                    if has(m - 2):
                        wait_tiles(dve, y_rs_ready, m, plus=-1)
                    dve.tensor_scalar(y_ve_buf[:, m.c % 2, :], y_mv_buf[:, m.c % U, 1:2], EPS, None, ALU.add).then_inc(y_ve, 1)
                if has(g):
                    wait_tiles(dve, yn_ready, g, plus=1)
                    if has(g - 2):
                        wait_tiles(dve, res_ready, g, plus=-1)
                    dve.tensor_tensor(yg[:, g.c % 2, :], yn[:, g.c % U, :], gamma_all[:], ALU.mult).then_inc(yg_ready, 1)
                if has(n):
                    wait_tiles(dve, y_rs_ready, n, plus=1)
                    if has(n - 2):
                        wait_tiles(dve, yn_ready, n, plus=-1)
                    dve.tensor_scalar(nb_y[:, n.c % 2, :], y_mv_buf[:, n.c % U, 0:1], y_rs[:, n.c % U, :], -1.0, ALU.mult,
                                      ALU.mult).then_inc(nb_y_ready, 1)
                if has(a):
                    wait_apart(dve, (y_done, a, 1))
                    dve.bn_stats(bn_y[:, a.c % 2, :], y[:, a.c % U, :]).then_inc(y_bn, 1)

            pipeline(dve, 8, T - 1, T + 3, output)


_INS = ["x", "dst_src", "L0_gnn_weight", "L0_gnn_attn_l", "L0_gnn_attn_r", "L0_ffn_gate_w", "L0_ffn_gate_b", "L0_ffn_w1",
        "L0_ffn_b1", "L0_ffn_w2", "L0_ffn_b2", "L0_ffn_gamma", "L0_ffn_beta"]


def kernel(**inputs):
    import numpy as _np
    import concourse.bacc as _bacc
    from concourse import mybir as _mybir
    from concourse.bass_utils import run_bass_kernel_spmd as _run

    given = dict(inputs)
    given["x"] = _np.concatenate([_np.asarray(inputs["x"]), _np.zeros((NP - N, C), _np.float32)])
    edges = _np.zeros((P, T, 2), _np.int32)
    for at, name in ((0, "dst"), (1, "src")):
        whole = _np.zeros(NP, _np.int32)
        whole[:N] = _np.asarray(inputs[name])[:N]
        edges[:, :, at] = whole.reshape(P, T)
    given["dst_src"] = edges

    nc = _bacc.Bacc("TRN2", target_bir_lowering=False, num_devices=1)
    arrays, args = {}, []
    for name in _INS:
        a = _np.ascontiguousarray(given[name])
        arrays[f"in_{name}_dram"] = a
        args.append(nc.dram_tensor(f"in_{name}_dram", a.shape, _mybir.dt.from_np(a.dtype), kind="ExternalInput").ap())
    args.append(nc.dram_tensor("out_0_dram", (NP, C), F32, kind="ExternalOutput").ap())
    bass_gnn_moe(nc, *args)
    r = _run(nc, [arrays], core_ids=[0])
    return r.results[0]["out_0_dram"][:N]
```

```python
from contextlib import ExitStack, nullcontext

import concourse.bass as bass
from concourse import mybir

F32 = mybir.dt.float32
BF16 = mybir.dt.bfloat16
I32 = mybir.dt.int32
ALU = mybir.AluOpType
ACT = mybir.ActivationFunctionType
AX_X = mybir.AxisListType.X

P = 128
N = 6250
T = -(-N // P)
NP = T * P
TG = -(-T // 4) * 4
C = 256
KC = C // P
HEADS, DH = 4, 64
E, K, F = 16, 2, 512
FC = F // P
EPS = 1e-5
SLOPE = 0.01
XW = C + HEADS
BLOCKS = (K * NP + E * (P - 1)) // P
FULL_BLOCKS = K * NP // P
RING = 4
U = 8
G = 7
NO_ROW = 1 << 20


class Tile:

    def __init__(self, c, i=None):
        self.c, self.i = c, i

    def __add__(self, n):
        return Tile(self.c + n, self.i)

    def __sub__(self, n):
        return Tile(self.c - n, self.i)

    def value(self, times=1, plus=0):
        c = self.c * times + plus
        return c if self.i is None else self.i * (U * times) + c

    def groups(self, n):
        c = self.c // n + 1
        return c if self.i is None else self.i * (U // n) + c

    def least(self, times=1, plus=0):
        return self.c * times + plus


def wait_tiles(eng, sem, tile, times=1, plus=0):
    if tile.i is None and tile.least(times, plus) <= 0:
        return
    assert tile.least(times, plus) > 0
    eng.wait_ge(sem, tile.value(times, plus))


def steps(eng, first, last, body):
    rounds = (last - first + 1) // U
    if rounds > 1:
        with eng.Fori(0, rounds) as i:
            for u in range(U):
                body(Tile(first + u, i))
        first += rounds * U
    for t in range(first, last + 1):
        body(Tile(t))


def pipeline(eng, first_full, last_full, end, body):
    for t in range(first_full):
        body(Tile(t))
    steps(eng, first_full, last_full, body)
    for t in range(last_full + 1, end + 1):
        body(Tile(t))


def bass_gnn_moe(nc, x, dst_src, weight, attn_l, attn_r, gate_w, gate_b, w1, b1, w2, b2, gamma, beta, out):
    ctx = ExitStack()
    with ctx:
        def sb(name, shape, dt=F32):
            return ctx.enter_context(nc.sbuf_tensor(name, shape, dt))

        def sem(name):
            return ctx.enter_context(nc.semaphore(name))

        def sems(name, n):
            return [sem(f"{name}{i}") for i in range(n)]

        z_rows = nc.dram_tensor("z_rows", (NP, C), F32, kind="Internal").ap()
        moe_rows = nc.dram_tensor("moe_rows", (K * NP, C), F32, kind="Internal").ap()
        z_tiles = z_rows.rearrange("(p j) c -> p j c", j=T)
        x_tiles = x.rearrange("(p j) c -> p j c", j=T)
        out_tiles = out.rearrange("(p j) c -> p j c", j=T)
        moe_tiles = moe_rows.rearrange("(p j k) c -> p j (k c)", j=T, k=K)
        w1_view = w1.rearrange("e (k p) f -> e p k f", p=P)

        ident = sb("ident", [P, P])
        before = sb("before", [P, P], BF16)
        ones = sb("ones", [P, P], BF16)
        iota_rep = sb("iota_rep", [P, P, G], BF16)
        iota_blk = sb("iota_blk", [P, BLOCKS])
        iota_e16 = sb("iota_e16", [P, E, T], BF16)
        row_no = sb("row_no", [P, 1])
        choice_no = sb("choice_no", [P, T * K], BF16)
        minus_half = sb("minus_half", [P, 3])
        w_gnn = sb("w_gnn", [P, KC, XW])
        w_gnn_l = sb("w_gnn_l", [P, KC, HEADS])
        wg = sb("wg", [P, KC, E])
        bg = sb("bg", [P, E])
        w2_all = sb("w2_all", [P, E, FC * C])
        b1_rows = sb("b1_rows", [E * FC, P])
        b1_cols = sb("b1_cols", [P, E * FC])
        b2_all = sb("b2_all", [P, E, C])
        gamma_all = sb("gamma_all", [P, C])
        beta_all = sb("beta_all", [P, C])
        x2_all = sb("x2_all", [P, T, C])
        logits = sb("logits", [P, E, T])
        gate = sb("gate", [P, K, T])
        rs = sb("rs", [P, T + 6, 3])
        nb_z = sb("nb_z", [P, T])
        src_dst = sb("src_dst", [P, TG, 2], I32)
        idx = sb("idx", [P, 2 * RING, 2], I32)
        x_sd = sb("x_sd", [P, RING, 2, C])
        bn = sb("bn", [P, 3, 6])
        mv = sb("mv", [P, RING, 3, 2])
        ve = sb("ve", [P, 2, 3])
        nb = sb("nb", [P, 2, 2])
        z_sd = sb("z_sd", [P, 2, 2, C])
        zT_sd = sb("zT_sd", [P, 2, 2 * KC * P])
        x_own = sb("x_own", [P, 2, C])
        z_last = sb("z_last", [P, RING, C])
        score = sb("score", [P, HEADS])
        leaky = sb("leaky", [P, HEADS])
        top = sb("top", [P, 1])
        centred = sb("centred", [P, 2, HEADS])
        prob = sb("prob", [P, 2, HEADS])
        psum_e = sb("psum_e", [P, 2, 1])
        rsum = sb("rsum", [P, 1])
        parts = sb("parts", [P, 2, C])
        zT = sb("zT", [P, 2, KC * P])
        w1_sb = sb("w1_sb", [P, RING, KC, F])
        z_in = sb("z_in", [P, RING, C])
        zT_in = sb("zT_in", [P, 2, KC * P])
        hT = sb("hT", [P, 2, F])
        moe_out = sb("moe_out", [P, RING, C])
        g_idx = sb("g_idx", [P, RING, 1], I32)
        s_idx = sb("s_idx", [P, RING, 1], I32)
        token_of = sb("token_of", [P, BLOCKS], I32)
        dest_of = sb("dest_of", [P, BLOCKS], I32)
        expert_of = sb("expert_of", [P, BLOCKS], I32)

        bank = [ctx.enter_context(nc.psum_tensor(f"bank{i}", [P, 512], F32)) for i in range(8)]

        n_te = T * E
        work = w1_sb[:].rearrange("p u k f -> p (u k f)")
        work_b = work.bitcast(BF16)

        def by_expert(buffer, at):
            return buffer[:, at * n_te:(at + 1) * n_te].rearrange("p (e t) -> p e t", t=T)

        hit0, hit1, equal, lowest = (by_expert(work_b, i) for i in range(4))
        product, rest = (by_expert(work, i) for i in (2, 3))
        running = by_expert(zT_sd[:].rearrange("p u n -> p (u n)"), 0)
        n_lo, n_blk = P * G, BLOCKS * G
        lo_hot = work_b[:, 0:2 * n_lo].rearrange("p (u b g) -> p u b g", u=2, g=G)
        blk_hot = work_b[:, 2 * n_lo:2 * n_lo + 6 * n_blk].rearrange("p (u s b g) -> p u s b g", u=2, s=3, g=G)
        attn = work[:, 0:2 * C].rearrange("p (s c) -> p s c", s=2)
        attn_prod = work[:, 2 * C:(2 + KC) * C].rearrange("p (k c) -> p k c", k=KC)
        small = hT[:].rearrange("p u f -> p (u f)")
        m0 = small[:, 0:T]
        m1 = small[:, T:2 * T]
        gap = small[:, 2 * T:3 * T]
        egap = small[:, 3 * T:4 * T]
        slot = small[:, 4 * T:6 * T]
        first_slot = small[:, 6 * T:6 * T + E]
        diagonal = small[0:E, 6 * T + E:6 * T + 2 * E]
        blocks_col = small[0:E, 6 * T + 2 * E:6 * T + 2 * E + 1]
        index = sb("index", [P, K, T], BF16)
        row_ends = sb("row_ends", [P, 1 + E])
        rowsum_b = sb("rowsum_b", [P, E], BF16)
        cnt_i = sb("cnt_i", [P, E], I32)
        nblk = sb("nblk", [P, E])
        zeros_e = sb("zeros_e", [P, E])
        blocks_to = sb("blocks_to", [P, E])
        slot_i = sb("slot_i", [P, T * K], I32)
        part_i = sb("part_i", [P, 2, T * K], I32)
        part_b = sb("part_b", [P, 2, T * K], BF16)
        past = sb("past", [E, BLOCKS], BF16)
        row_f = sb("row_f", [P, BLOCKS])
        code_f = sb("code_f", [P, BLOCKS])
        empty_f = sb("empty_f", [P, BLOCKS])
        dest_f = sb("dest_f", [P, BLOCKS])
        dest_g = sb("dest_g", [P, BLOCKS], I32)
        exp_f = sb("exp_f", [P, BLOCKS])
        used_blocks = sb("used_blocks", [P, 1], I32)
        moe_in = x_sd[:].rearrange("p u s c -> p u (s c)")
        gate_diag = work[:, 0:RING * K * P].rearrange("p (u k q) -> p u k q", u=RING, k=K)
        yn = zT_sd[:].rearrange("p u (s c) -> p (u s) c", c=C)
        yg = parts
        y_ve_buf = sb("y_ve_buf", [P, 2, 1])
        y_rs = sb("y_rs", [P, RING, 1])
        nb_y = sb("nb_y", [P, RING, 1])
        y_mv_buf = sb("y_mv_buf", [P, RING, 2])
        bn_y = sb("bn_y", [P, 2, 6])
        z_own = z_last
        res = moe_out

        def rows_at(tile):
            u = tile.c % (2 * RING)
            if u < RING:
                return x_sd[:, u, :, :]
            return w1_sb[:, RING // 2:RING].rearrange("p a k f -> p (a k) f").rearrange("p b (s c) -> p b s c", s=2)[:, u - RING]

        idx_loaded = sem("idx_loaded")
        gnn_w_loaded = sem("gnn_w_loaded")
        gate_loaded = sem("gate_loaded")
        consts_loaded = sem("consts_loaded")
        w2_loaded = sem("w2_loaded")
        const_step = sem("const_step")
        consts_made = sem("consts_made")
        iotas_made = sem("iotas_made")
        fold_step = sem("fold_step")
        gnn_w_ready = sem("gnn_w_ready")
        b1_turned = sem("b1_turned")
        b1_ready = sem("b1_ready")
        idx_copied = sem("idx_copied")
        gathered = sems("gathered", 2 * RING)
        own_loaded = sems("own_loaded", 2)
        bn_d = sem("bn_d")
        bn_s = sem("bn_s")
        mv_d = sem("mv_d")
        mv_s = sem("mv_s")
        bn_r = sem("bn_r")
        mv_r = sem("mv_r")
        nb_z_ready = sem("nb_z_ready")
        ve_ready = sem("ve_ready")
        rs_ready = sem("rs_ready")
        nb_ready = sem("nb_ready")
        norm_ready = sem("norm_ready")
        turned = sem("turned")
        turned_copied = sem("turned_copied")
        xt_ready = sem("xt_ready")
        score_kept = sem("score_kept")
        score_leaky = sem("score_leaky")
        score_top = sem("score_top")
        score_ready = sem("score_ready")
        prob_ready = sem("prob_ready")
        parts_ready = sem("parts_ready")
        rsum_ready = sem("rsum_ready")
        heads_summed = sem("heads_summed")
        x2_ready = sem("x2_ready")
        z_ready = sem("z_ready")
        z_stored = sems("z_stored", RING)
        z_turned = sem("z_turned")
        zT_copied = sem("zT_copied")
        logits_done = sem("logits_done")
        logits_kept = sem("logits_kept")
        route = sem("route")
        gap_ready = sem("gap_ready")
        egap_ready = sem("egap_ready")
        rowsum_ready = sem("rowsum_ready")
        counts_done = sem("counts_done")
        past_ready = sem("past_ready")
        expert_counted = sem("expert_counted")
        expert_of_ready = sem("expert_of_ready")
        equal_ready = sem("equal_ready")
        row_hot_ready = sem("row_hot_ready")
        hot_ready = sem("hot_ready")
        hot_used = sem("hot_used")
        tables_ready = sem("tables_ready")
        w1_loaded = sems("w1_loaded", 2)
        g_idx_copied = sem("g_idx_copied")
        z_gathered = sems("z_gathered", RING)
        z_in_turned = sem("z_in_turned")
        zT_in_ready = sem("zT_in_ready")
        hidden_done = sem("hidden_done")
        hT_ready = sem("hT_ready")
        expert_done = sem("expert_done")
        moe_ready = sem("moe_ready")
        s_idx_ready = sem("s_idx_ready")
        moe_stored = sems("moe_stored", RING)
        moe_loaded = sems("moe_loaded", RING)
        z_own_ready = sem("z_own_ready")
        beta_added = sem("beta_added")
        diag_ready = sem("diag_ready")
        y_done = sem("y_done")
        y_bn = sem("y_bn")
        y_mv = sem("y_mv")
        y_ve = sem("y_ve")
        y_rs_ready = sem("y_rs_ready")
        yn_ready = sem("yn_ready")
        nb_y_ready = sem("nb_y_ready")
        yg_ready = sem("yg_ready")
        res_ready = sem("res_ready")
        out_stored = sems("out_stored", RING)

        block = ctx.enter_context(nc.Block())

        def row(buffer, tile):
            if tile.i is None:
                return buffer[:, tile.c, :]
            return buffer[:, bass.ds(tile.value(), 1), :].rearrange("p o c -> p (o c)")

        def col(buffer, tile):
            return buffer[:, bass.ds(tile.value(), 1)]

        def rs_row(tile, s):
            return row(rs, tile)[:, s:s + 1]

        def expert(eng, tile):
            return eng.value_load(expert_of[0:1, bass.ds(tile.value(), 1)], min_val=0, max_val=E - 1)

        def blocks_used(eng):
            return eng.value_load(used_blocks[0:1, 0:1], min_val=FULL_BLOCKS, max_val=BLOCKS)

        def if_used(eng, used, tile):
            return nullcontext() if tile.i is not None or tile.c < FULL_BLOCKS else eng.If(used > tile.c)

        def has(tile, n=T):
            return tile.i is not None or 0 <= tile.c < n

        def wait_filled(eng, ring, tile, each=16, used=0):
            n = each * (tile.c // len(ring) + 1 - used)
            assert n > 0
            eng.wait_ge(ring[tile.c % len(ring)], n if tile.i is None else tile.i * (each * U // len(ring)) + n)

        def wait_apart(eng, *waits):
            values = [t.value(1, plus) if t is not None else plus for _, t, plus in waits]
            values = [v if isinstance(v, int) else eng.to_reg(v) for v in values]
            eng.wait_ge(consts_made, 1)
            for (sem_, _, _), value in zip(waits, values):
                eng.wait_ge(sem_, value)

        B_FULL, B_LAST, B_END = 14, T - 1, T + 12
        POWS = T + 6
        HOTS = T * K // G

        @block.sync
        def _(sp):
            sp.dma_start(src_dst[:], dst_src).then_inc(idx_loaded, 16)
            sp.dma_start(w_gnn[:, :, 0:C], weight.rearrange("(k p) n -> p k n", p=P)).then_inc(gnn_w_loaded, 16)
            for a, at in ((attn_l, 0), (attn_r, 1)):
                sp.dma_start(attn[:, at, :], a.rearrange("(o h) d -> o (h d)", o=1).to_broadcast([P, C])).then_inc(gnn_w_loaded, 16)
            sp.dma_start(wg[:], gate_w.rearrange("(k p) e -> p k e", p=P)).then_inc(gate_loaded, 16)
            sp.dma_start(bg[:], gate_b.rearrange("(o e) -> o e", o=1).to_broadcast([P, E])).then_inc(gate_loaded, 16)

            def attention(t):
                own, norm = t - 4, t - 9
                if has(own):
                    if has(own - 2):
                        wait_tiles(sp, x2_ready, own, plus=-1)
                    sp.dma_start(x_own[:, own.c % 2, :], row(x_tiles, own)).then_inc(own_loaded[own.c % 2], 16)
                if has(norm):
                    wait_tiles(sp, z_ready, norm, plus=1)
                    sp.dma_start(row(z_tiles, norm), z_last[:, norm.c % RING, :]).then_inc(z_stored[norm.c % RING], 16)

            def attention_and_w2(t):
                attention(t)
                if t.c % 2:
                    e = t.i * (U // 2) + (t.c - B_FULL) // 2
                    sp.dma_start(w2_all[:, bass.ds(e, 1), :].rearrange("p o (c n) -> p (o c) n", n=C),
                                 w2[bass.ds(e, 1)].rearrange("o (c p) n -> p (o c) n", p=P)).then_inc(w2_loaded, 16)

            for t in range(B_FULL):
                attention(Tile(t))
                if t == 4:
                    sp.dma_start(b1_rows[:], b1.rearrange("e (c f) -> (e c) f", f=P)).then_inc(consts_loaded, 16)
                    sp.dma_start(gamma_all[:], gamma.rearrange("(o c) -> o c", o=1).to_broadcast([P, C])).then_inc(consts_loaded, 16)
                    sp.dma_start(beta_all[:], beta.rearrange("(o c) -> o c", o=1).to_broadcast([P, C])).then_inc(consts_loaded, 16)
                if t == 8:
                    sp.dma_start(b2_all[:].rearrange("p e c -> p (e c)"),
                                 b2.rearrange("(o e) c -> o (e c)", o=1).to_broadcast([P, E * C])).then_inc(consts_loaded, 16)
            steps(sp, B_FULL, B_FULL + 2 * E - 1, attention_and_w2)
            for t in range(B_FULL + 2 * E, B_END + 1):
                attention(Tile(t))

            sp.wait_ge(expert_of_ready, 1)
            sp.wait_ge(hot_used, HOTS)

            used = blocks_used(sp)

            def load_w1(t):
                u = t.c % 2
                e = expert(sp, t)
                new = w1_view[bass.ds(e, 1)].rearrange("o p k f -> p (o k) f")
                if has(t - 2, BLOCKS):
                    old = expert(sp, t - 2)
                    wait_apart(sp, (hidden_done, t, -1))
                    sp.dma_start(w1_sb[:, u], new, cond=(e != old)).then_inc(w1_loaded[u], 16)
                else:
                    sp.dma_start(w1_sb[:, u], new).then_inc(w1_loaded[u], 16)

            def experts(t):
                with if_used(sp, used, t):
                    load_w1(t)

            pipeline(sp, RING, FULL_BLOCKS - 1, BLOCKS - 1, experts)

            for b in range(FULL_BLOCKS - RING, BLOCKS):
                with if_used(sp, used, Tile(b)):
                    wait_filled(sp, moe_stored, Tile(b))

            def output(t):
                load, store = t, t - 11
                if has(load):
                    if has(load - RING):
                        wait_tiles(sp, y_done, load, plus=1 - RING)
                    sp.dma_start(moe_in[:, load.c % RING, :], row(moe_tiles, load)).then_inc(moe_loaded[load.c % RING], 16)
                if has(store):
                    wait_tiles(sp, res_ready, store, plus=1)
                    sp.dma_start(row(out_tiles, store), res[:, store.c % RING, :]).then_inc(out_stored[store.c % RING], 16)

            pipeline(sp, 13, T - 1, T + 10, output)
            for u in range(RING):
                sp.wait_ge(out_stored[u], 16 * len(range(u, T, RING)))

        @block.gpsimd
        def _(pool):
            made = [0]

            def link(ins):
                made[0] += 1
                ins.then_inc(const_step, 1)
                pool.wait_ge(const_step, made[0])

            link(pool.memset(ident[:], 0.0))
            link(pool.affine_select(out=ident[:], in_=ident[:], compare_op=ALU.not_equal, fill=1.0, base=0,
                                    pattern=[[-1, P]], channel_multiplier=1))
            link(pool.memset(minus_half[:], -0.5))
            link(pool.memset(ones[:], 1.0))
            link(pool.affine_select(out=before[:], in_=ones[:], compare_op=ALU.is_gt, fill=0.0, base=0,
                                    pattern=[[1, P]], channel_multiplier=-1))
            pool.engine_nop().then_inc(consts_made, 1)
            pool.wait_ge(idx_loaded, 16)

            def copy_rows(t):
                at = t.c % (2 * RING)
                pool.tensor_copy(idx[:, at:at + RING, :], src_dst[:, bass.ds(t.value(), RING), :]).then_inc(idx_copied, 1)

            def attention(t):
                if has(t):
                    u = t.c % RING
                    if u == 3 and (t.i is not None or t.c + 1 < T):
                        if has(t - 7):
                            for last in range(4, 8):
                                wait_filled(pool, gathered, t - last, each=32)
                        copy_rows(t + 1)
                    waits = []
                    if has(t - 2 * RING):
                        waits.append((norm_ready, t, 1 - 2 * RING))
                    if u == 0:
                        waits.append((idx_copied, None, t.groups(RING)))
                    if waits:
                        wait_apart(pool, *waits)
                    at = t.c % (2 * RING)
                    for s in range(2):
                        pool.indirect_dma_start(
                            rows_at(t)[:, s, :], None, x, bass.IndirectOffsetOnAxis(ap=idx[:, at, s:s + 1], axis=0),
                            bounds_check=NP - 1).then_inc(gathered[at], 16)
                p = t - 2
                if has(p, POWS):
                    wait_tiles(pool, ve_ready, p, plus=1)
                    pool.tensor_tensor(row(rs, p), ve[:, p.c % 2, :], minus_half[:], ALU.pow).then_inc(rs_ready, 1)

            copy_rows(Tile(0))
            pipeline(pool, B_FULL, B_LAST, B_END, attention)

            for to, pattern, base_, by_row in (
                    (iota_e16, [[1, E], [0, T]], -E, 0), (iota_blk, [[1, BLOCKS]], 0, 0), (row_no, [[0, 1]], 0, 1),
                    (iota_rep, [[1, P], [0, G]], 0, 0), (choice_no, [[1, K], [K, T]], 1, 0)):
                pool.iota(to[:], pattern, base=base_, channel_multiplier=by_row,
                          allow_small_or_imprecise_dtypes=True).then_inc(iotas_made, 1)

            pool.wait_ge(tables_ready, 1)
            for u in range(RING):
                pool.wait_ge(z_stored[u], 16 * len(range(u, T, RING)))

            pool.wait_ge(expert_of_ready, 1)
            used = blocks_used(pool)

            def gather(t):
                u = t.c % RING
                if has(t - RING, BLOCKS):
                    wait_tiles(pool, z_in_turned, t, plus=1 - RING)
                pool.tensor_copy(g_idx[:, u, :], col(token_of, t)).then_inc(g_idx_copied, 1)
                wait_apart(pool, (g_idx_copied, t, 1))
                pool.indirect_dma_start(
                    z_in[:, u, :], None, z_rows, bass.IndirectOffsetOnAxis(ap=g_idx[:, u, :], axis=0),
                    bounds_check=NP - 1).then_inc(z_gathered[u], 16)

            def scatter(t):
                u = t.c % RING
                wait_apart(pool, (s_idx_ready, t, 1), (moe_ready, t, 1))
                pool.indirect_dma_start(
                    moe_rows, bass.IndirectOffsetOnAxis(ap=s_idx[:, u, :], axis=0), moe_out[:, u, :], None,
                    bounds_check=K * NP - 1, oob_is_err=False).then_inc(moe_stored[u], 16)

            def exchange(t):
                if has(t, BLOCKS):
                    with if_used(pool, used, t):
                        gather(t)
                if has(t - 4, BLOCKS):
                    with if_used(pool, used, t - 4):
                        scatter(t - 4)

            pipeline(pool, 4, FULL_BLOCKS - 1, BLOCKS + 3, exchange)

            def output(t):
                p, s = t - 1, t - 6
                if has(p):
                    wait_tiles(pool, y_ve, p, plus=1)
                    if has(p - RING):
                        wait_tiles(pool, yn_ready, p, plus=1 - RING)
                    pool.tensor_tensor(y_rs[:, p.c % RING, :], y_ve_buf[:, p.c % 2, :], minus_half[:, 0:1], ALU.pow).then_inc(y_rs_ready, 1)
                if has(s):
                    wait_apart(pool, (beta_added, s, 1), (yg_ready, s, 1))
                    if has(s - RING):
                        wait_filled(pool, out_stored, s, used=1)
                    pool.tensor_tensor(res[:, s.c % RING, :], yg[:, s.c % 2, :], row(x2_all, s), ALU.add).then_inc(res_ready, 1)

            pipeline(pool, 10, T - 1, T + 5, output)

        @block.tensor
        def _(pe):
            pe.wait_ge(consts_made, 1)
            pe.wait_ge(gate_loaded, 32)

            def attention(t):
                xt, lg, tr, tz, hs = t - 5, t - 12, t - 3, t - 10, t - 7
                if has(hs):
                    wait_tiles(pe, parts_ready, hs, plus=1)
                    if has(hs - 1):
                        wait_tiles(pe, x2_ready, hs)
                    for h in range(HEADS):
                        mm = pe.matmul(bank[7][:, 0:DH], ident[:], parts[:, hs.c % 2, h * DH:(h + 1) * DH],
                                       start=(h == 0), stop=(h == HEADS - 1))
                    mm.then_inc(heads_summed, 1)
                if has(xt):
                    if xt.c == 0 and t.i is None:
                        pe.wait_ge(gnn_w_ready, 1)
                    wait_tiles(pe, turned_copied, xt, plus=1)
                    if has(xt - 2):
                        wait_tiles(pe, parts_ready, xt, plus=-1)
                        wait_tiles(pe, score_kept, xt, plus=-1)
                    u, to = xt.c % 2, bank[2 + xt.c % 2]
                    for k in range(KC):
                        pe.matmul(to[:, 0:XW], zT_sd[:, u, k * P:(k + 1) * P], w_gnn[:, k, :],
                                  start=(k == 0), stop=False)
                    for k in range(KC):
                        mm = pe.matmul(to[:, C:XW], zT_sd[:, u, (KC + k) * P:(KC + k + 1) * P],
                                       w_gnn_l[:, k, :], start=False, stop=(k == KC - 1))
                    mm.then_inc(xt_ready, 1)
                if has(tz):
                    wait_tiles(pe, z_ready, tz, plus=1)
                    if has(tz - 2):
                        wait_tiles(pe, zT_copied, tz, plus=-1)
                    u = tz.c % 2
                    for k in range(KC):
                        mm = pe.transpose(bank[4 + u][:, k * P:(k + 1) * P], z_last[:, tz.c % RING, k * P:(k + 1) * P], ident[:])
                    mm.then_inc(z_turned, 1)
                if has(lg):
                    wait_tiles(pe, zT_copied, lg, plus=1)
                    if has(lg - 1):
                        wait_tiles(pe, logits_kept, lg)
                    u = lg.c % 2
                    for k in range(KC):
                        mm = pe.matmul(bank[6][:, 0:E], zT[:, u, k * P:(k + 1) * P], wg[:, k, :],
                                       start=(k == 0), stop=(k == KC - 1))
                    mm.then_inc(logits_done, 1)
                if has(tr):
                    wait_tiles(pe, norm_ready, tr, plus=1)
                    if has(tr - 2):
                        wait_tiles(pe, turned_copied, tr, plus=-1)
                    u = tr.c % 2
                    for s in range(2):
                        for k in range(KC):
                            q = (s * KC + k) * P
                            mm = pe.transpose(bank[u][:, q:q + P], z_sd[:, u, s, k * P:(k + 1) * P], ident[:])
                    mm.then_inc(turned, 1)

            pipeline(pe, B_FULL, B_LAST, B_END, attention)

            pe.wait_ge(consts_loaded, 64)
            pe.wait_ge(turned_copied, T)
            pe.transpose(bank[0][:, 0:E * FC], b1_rows[:], ident[0:E * FC, 0:E * FC]).then_inc(b1_turned, 1)

            pe.wait_ge(rowsum_ready, 1)
            pe.matmul(bank[7][:, 0:E], before[:], rowsum_b[:], start=True, stop=True)
            pe.matmul(bank[7][:, E:2 * E], ones[:], rowsum_b[:], start=True, stop=True).then_inc(counts_done, 1)

            pe.wait_ge(past_ready, 1)
            pe.matmul(bank[7][:, 2 * E:2 * E + BLOCKS], ones[0:E, :], past[:], start=True, stop=True).then_inc(expert_counted, 1)

            def tables(h):
                wait_tiles(pe, row_hot_ready, h, plus=1)
                wait_tiles(pe, hot_ready, h, plus=1)
                first, last = h.i is None and h.c == 0, h.i is None and h.c == HOTS - 1
                for g in range(G):
                    mm = pe.matmul(bank[6][:, 0:2 * BLOCKS].rearrange("p (s b) -> p s b", s=2), lo_hot[:, h.c % 2, :, g],
                                   blk_hot[:, h.c % 2, 1:3, :, g], start=(first and g == 0), stop=(last and g == G - 1))
                mm.then_inc(hot_used, 1)

            pipeline(pe, 1, HOTS - 2, HOTS - 1, tables)

            def turn(t):
                u = t.c % 2
                wait_filled(pe, z_gathered, t)
                if has(t - 2, BLOCKS):
                    wait_tiles(pe, zT_in_ready, t, plus=-1)
                for k in range(KC):
                    mm = pe.transpose(bank[u][:, k * P:(k + 1) * P], z_in[:, t.c % RING, k * P:(k + 1) * P], ident[:])
                mm.then_inc(z_in_turned, 1)

            def hidden(t):
                u = t.c % 2
                wait_tiles(pe, zT_in_ready, t, plus=1)
                wait_filled(pe, w1_loaded, t)
                if has(t - 2, BLOCKS):
                    wait_tiles(pe, hT_ready, t, plus=-1)
                for f in range(FC):
                    for k in range(KC):
                        mm = pe.matmul(bank[2 + u][:, f * P:(f + 1) * P], w1_sb[:, t.c % 2, k, f * P:(f + 1) * P],
                                       zT_in[:, u, k * P:(k + 1) * P], start=(k == 0), stop=(k == KC - 1))
                mm.then_inc(hidden_done, 1)

            def second(t):
                u = t.c % 2
                e = expert(pe, t)
                wait_tiles(pe, hT_ready, t, plus=1)
                if has(t - 2, BLOCKS):
                    wait_tiles(pe, moe_ready, t, plus=-1)
                for f in range(FC):
                    mm = pe.matmul(bank[4 + u][:, 0:C], hT[:, u, f * P:(f + 1) * P],
                                   w2_all[:, bass.ds(e, 1), f * C:(f + 1) * C].rearrange("p o c -> p (o c)"),
                                   start=(f == 0), stop=(f == FC - 1))
                mm.then_inc(expert_done, 1)

            pe.wait_ge(expert_of_ready, 1)
            used = blocks_used(pe)
            turn(Tile(0))
            pe.wait_ge(w2_loaded, 16 * E)

            def experts(t):
                for stage, of in ((hidden, t), (turn, t + 1), (second, t - 1)):
                    if has(of, BLOCKS):
                        with if_used(pe, used, of):
                            stage(of)

            pipeline(pe, 4, FULL_BLOCKS - 2, BLOCKS, experts)

            def output(t):
                u, y = t.c % RING, bank[t.c % 8][:, 0:C]
                if has(t - 8):
                    wait_tiles(pe, yn_ready, t, plus=-7)
                wait_tiles(pe, diag_ready, t, plus=1)
                wait_tiles(pe, z_own_ready, t, plus=1)
                pe.matmul(y, ident[:], z_own[:, u, :], start=True, stop=False)
                wait_filled(pe, moe_loaded, t)
                for k in range(K):
                    mm = pe.matmul(y, gate_diag[:, u, k, :], moe_in[:, u, k * C:(k + 1) * C], start=False, stop=(k == K - 1))
                mm.then_inc(y_done, 1)

            pipeline(pe, 8, T - 1, T - 1, output)

        @block.scalar
        def _(act):
            def attention(t):
                cp, zs, cz, sm = t - 4, t - 3, t - 11, t - 6
                if has(zs):
                    wait_tiles(act, nb_ready, zs, plus=1)
                    wait_tiles(act, rs_ready, zs, plus=1)
                    if has(zs - 2):
                        wait_tiles(act, turned, zs, plus=-1)
                    for s in range(2):
                        a = act.activation(z_sd[:, zs.c % 2, s, :], rows_at(zs)[:, s, :], ACT.Identity,
                                           bias=nb[:, zs.c % 2, s:s + 1], scale=rs_row(zs, s))
                    a.then_inc(norm_ready, 1)
                if has(sm):
                    u = sm.c % 2
                    wait_tiles(act, score_ready, sm, plus=1)
                    if has(sm - 2):
                        wait_tiles(act, heads_summed, sm, plus=-1)
                        wait_tiles(act, rsum_ready, sm, plus=-1)
                    act.activation(prob[:, u, :], centred[:, u, :], ACT.Exp, accum_out=psum_e[:, u, :]).then_inc(prob_ready, 1)
                    wait_tiles(act, prob_ready, sm, plus=1)
                    for h in range(HEADS):
                        a = act.activation(parts[:, u, h * DH:(h + 1) * DH], bank[2 + u][:, h * DH:(h + 1) * DH],
                                           ACT.Copy, scale=prob[:, u, h:h + 1])
                    a.then_inc(parts_ready, 1)
                if has(cp):
                    wait_tiles(act, turned, cp, plus=1)
                    if has(cp - 2):
                        wait_tiles(act, xt_ready, cp, plus=-1)
                    act.copy(zT_sd[:, cp.c % 2, :], bank[cp.c % 2][:, :]).then_inc(turned_copied, 1)
                if has(cz):
                    wait_tiles(act, z_turned, cz, plus=1)
                    if has(cz - 2):
                        wait_tiles(act, logits_done, cz, plus=-1)
                    act.copy(zT[:, cz.c % 2, :], bank[4 + cz.c % 2][:, 0:C]).then_inc(zT_copied, 1)

            pipeline(act, B_FULL, B_LAST, B_END, attention)

            act.wait_ge(b1_turned, 1)
            act.copy(b1_cols[:], bank[0][:, 0:E * FC]).then_inc(b1_ready, 1)
            act.wait_ge(gap_ready, 1)
            act.activation(egap, gap, ACT.Exp).then_inc(egap_ready, 1)

            def row_hots(h):
                wait_tiles(act, equal_ready, h, plus=1)
                if has(h - 2, HOTS):
                    wait_tiles(act, hot_used, h, plus=-1)
                act.activation(blk_hot[:, h.c % 2, 1, :, :], blk_hot[:, h.c % 2, 0, :, :], ACT.Copy,
                               scale=row_no[:]).then_inc(row_hot_ready, 1)

            act.wait_ge(iotas_made, 5)
            pipeline(act, 2, HOTS - 1, HOTS - 1, row_hots)
            act.wait_ge(b1_ready, 1)
            act.wait_ge(expert_of_ready, 1)

            used = blocks_used(act)

            def relu(t):
                u = t.c % 2
                e = expert(act, t)
                wait_tiles(act, hidden_done, t, plus=1)
                if has(t - 2, BLOCKS):
                    wait_tiles(act, expert_done, t, plus=-1)
                for f in range(FC):
                    a = act.activation(hT[:, u, f * P:(f + 1) * P], bank[2 + u][:, f * P:(f + 1) * P], ACT.Relu,
                                       bias=b1_cols[:, bass.ds(e * FC + f, 1)])
                a.then_inc(hT_ready, 1)

            def experts(t):
                with if_used(act, used, t):
                    relu(t)

            pipeline(act, 4, FULL_BLOCKS - 1, BLOCKS - 1, experts)

            def output(t):
                z, a = t + 2, t - 4
                if has(z):
                    if has(z - RING):
                        wait_tiles(act, y_done, z, plus=1 - RING)
                    act.activation(z_own[:, z.c % RING, :], row(x2_all, z), ACT.Identity, bias=col(nb_z, z),
                                   scale=rs_row(z + 6, 2)).then_inc(z_own_ready, 1)
                    for k in range(K):
                        d = act.activation(gate_diag[:, z.c % RING, k, :], ident[:], ACT.Copy, scale=col(gate[:, k, :], z))
                    d.then_inc(diag_ready, 1)
                if has(a):
                    wait_tiles(act, nb_y_ready, a, plus=1)
                    if has(a - RING):
                        wait_tiles(act, yg_ready, a, plus=1 - RING)
                    act.activation(yn[:, a.c % RING, :], bank[a.c % 8][:, 0:C], ACT.Identity, bias=nb_y[:, a.c % RING, :],
                                   scale=y_rs[:, a.c % RING, :]).then_inc(yn_ready, 1)

            act.wait_ge(nb_z_ready, T)
            for t in (-2, -1):
                output(Tile(t))
            pipeline(act, 8, T - 3, T + 3, output)

        @block.vector
        def _(dve):
            dve.wait_ge(gnn_w_loaded, 48)
            folded = 0
            for s, dest in ((0, w_gnn_l[:, :, :]), (1, w_gnn[:, :, C:XW])):
                for k in range(KC):
                    ins = dve.tensor_tensor(attn_prod[:, k, :], w_gnn[:, k, 0:C], attn[:, s, :], ALU.mult)
                ins.then_inc(fold_step, 1)
                folded += 1
                dve.wait_ge(fold_step, folded)
                dve.tensor_reduce(dest, attn_prod.rearrange("p k (h d) -> p k h d", d=DH), AX_X, ALU.add).then_inc(fold_step, 1)
                folded += 1
                dve.wait_ge(fold_step, folded)
            dve.memset(zeros_e[:], 0.0)
            dve.memset(mv[:], 1.0).then_inc(gnn_w_ready, 1)
            dve.wait_ge(gnn_w_ready, 1)
            dve.wait_ge(gate_loaded, 32)

            def attention(t):
                st, nm, sc, rd, n2, lg = t - 2, t - 3, t - 6, t - 7, t - 9, t - 13
                if has(nm):
                    w = nm.c % RING
                    wait_tiles(dve, rs_ready, nm, plus=1)
                    if has(nm - 2):
                        wait_tiles(dve, norm_ready, nm, plus=-1)
                    dve.scalar_tensor_tensor(out=nb[:, nm.c % 2, :], in0=mv[:, w, 0:2, 0], scalar=-1.0,
                                             in1=row(rs, nm)[:, 0:2], op0=ALU.mult, op1=ALU.mult).then_inc(nb_ready, 1)
                if has(st):
                    wait_filled(dve, gathered, st, each=32)
                    dve.bn_stats(bn[:, 0, :], rows_at(st)[:, 0, :]).then_inc(bn_d, 1)
                if has(rd - 1):
                    wait_apart(dve, (bn_r, rd - 1, 1))
                    dve.bn_aggr(mv[:, (rd.c + 5) % RING, 2, :], bn[:, 2, :]).then_inc(mv_r, 1)
                if has(lg):
                    wait_tiles(dve, logits_done, lg, plus=1)
                    dve.tensor_tensor(logits[:, :, bass.ds(lg.value(), 1)].rearrange("p e o -> p (e o)"), bank[6][:, 0:E], bg[:], ALU.add).then_inc(logits_kept, 1)
                if has(sc):
                    u = sc.c % 2
                    wait_tiles(dve, xt_ready, sc, plus=1)
                    dve.tensor_copy(score[:], bank[2 + u][:, C:XW]).then_inc(score_kept, 1)
                if has(st):
                    dve.bn_stats(bn[:, 1, :], rows_at(st)[:, 1, :]).then_inc(bn_s, 1)
                if has(sc):
                    wait_tiles(dve, score_kept, sc, plus=1)
                    dve.scalar_tensor_tensor(out=leaky[:], in0=score[:], scalar=SLOPE, in1=score[:], op0=ALU.mult,
                                             op1=ALU.max).then_inc(score_leaky, 1)
                if has(st):
                    wait_apart(dve, (bn_d, st, 1))
                    dve.bn_aggr(mv[:, st.c % RING, 0, :], bn[:, 0, :]).then_inc(mv_d, 1)
                if has(sc):
                    wait_tiles(dve, score_leaky, sc, plus=1)
                    dve.tensor_reduce(top[:], leaky[:], AX_X, ALU.max).then_inc(score_top, 1)
                if has(st):
                    wait_apart(dve, (bn_s, st, 1))
                    dve.bn_aggr(mv[:, st.c % RING, 1, :], bn[:, 1, :]).then_inc(mv_s, 1)
                if has(sc):
                    wait_tiles(dve, score_top, sc, plus=1)
                    if has(sc - 2):
                        wait_tiles(dve, prob_ready, sc, plus=-1)
                    dve.tensor_scalar(centred[:, u, :], leaky[:], top[:], None, ALU.subtract).then_inc(score_ready, 1)
                if has(rd):
                    v = rd.c % 2
                    wait_tiles(dve, prob_ready, rd, plus=1)
                    dve.reciprocal(rsum[:], psum_e[:, v, :]).then_inc(rsum_ready, 1)
                if has(st, POWS):
                    if has(st):
                        wait_tiles(dve, mv_d, st, plus=1)
                        wait_tiles(dve, mv_s, st, plus=1)
                    if has(st - 6):
                        wait_tiles(dve, mv_r, st, plus=-5)
                    if has(st - 2, POWS):
                        wait_tiles(dve, rs_ready, st, plus=-1)
                    dve.tensor_scalar(ve[:, st.c % 2, :], mv[:, st.c % RING, :, 1], EPS, None, ALU.add).then_inc(ve_ready, 1)
                if has(rd):
                    wait_tiles(dve, rsum_ready, rd, plus=1)
                    wait_tiles(dve, heads_summed, rd, plus=1)
                    wait_filled(dve, own_loaded, rd)
                    dve.scalar_tensor_tensor(
                        out=row(x2_all, rd).rearrange("p (h d) -> p h d", h=HEADS),
                        in0=bank[7][:, 0:DH].rearrange("p (o d) -> p o d", o=1).to_broadcast([P, HEADS, DH]), scalar=rsum[:],
                        in1=x_own[:, v, :].rearrange("p (h d) -> p h d", h=HEADS), op0=ALU.mult,
                        op1=ALU.add).then_inc(x2_ready, 1)
                if has(n2):
                    w = (n2.c + 6) % RING
                    wait_tiles(dve, rs_ready, n2, plus=7)
                    dve.tensor_scalar(col(nb_z, n2), mv[:, w, 2, 0:1], rs_row(n2 + 6, 2), -1.0, ALU.mult,
                                      ALU.mult).then_inc(nb_z_ready, 1)
                    if has(n2 - RING):
                        wait_filled(dve, z_stored, n2, used=1)
                        wait_tiles(dve, z_turned, n2, plus=1 - RING)
                    dve.tensor_scalar(z_last[:, n2.c % RING, :], row(x2_all, n2), mv[:, w, 2, 0:1], rs_row(n2 + 6, 2),
                                      ALU.subtract, ALU.mult).then_inc(z_ready, 1)
                if has(rd):
                    wait_apart(dve, (x2_ready, rd, 1))
                    dve.bn_stats(bn[:, 2, :], row(x2_all, rd)).then_inc(bn_r, 1)

            pipeline(dve, B_FULL, B_LAST, B_END, attention)

            count = [0]

            def link(ins):
                count[0] += 1
                ins.then_inc(route, 1)
                dve.wait_ge(route, count[0])

            def over_e(a):
                return a.rearrange("p (o t) -> p o t", o=1).to_broadcast([P, E, T])

            def over_t(a):
                return a.rearrange("p (e o) -> p e o", o=1).to_broadcast([P, E, T])

            def by_tile(a):
                return a.rearrange("p e t -> p t e")

            dve.wait_ge(logits_kept, T)
            dve.wait_ge(iotas_made, 5)

            def pick(values, largest, lowest_index, hit):
                link(dve.tensor_reduce(largest, by_tile(values), AX_X, ALU.max))
                link(dve.tensor_tensor(equal, values, over_e(largest), ALU.is_equal))
                link(dve.tensor_tensor(lowest, equal, iota_e16[:], ALU.mult))
                link(dve.tensor_reduce(lowest_index, by_tile(lowest), AX_X, ALU.min))
                link(dve.tensor_tensor(hit, iota_e16[:], over_e(lowest_index), ALU.is_equal))

            pick(logits[:], m0, index[:, 0, :], hit0)
            link(dve.scalar_tensor_tensor(out=rest, in0=hit0, scalar=-3.0e38, in1=logits[:], op0=ALU.mult, op1=ALU.add))
            pick(rest, m1, index[:, 1, :], hit1)
            dve.tensor_tensor(gap, m1, m0, ALU.subtract).then_inc(gap_ready, 1)
            dve.memset(row_ends[:, 0:1], 0.0)
            link(dve.tensor_tensor_scan(running.rearrange("p e t -> p (e t)"), hit0.rearrange("p e t -> p (e t)"),
                                        hit1.rearrange("p e t -> p (e t)"), 0.0, ALU.add, ALU.add))
            link(dve.tensor_copy(row_ends[:, 1:1 + E], running[:, :, T - 1]))
            dve.tensor_tensor(rowsum_b[:], row_ends[:, 1:1 + E], row_ends[:, 0:E], ALU.subtract).then_inc(rowsum_ready, 1)
            dve.wait_ge(counts_done, 1)
            link(dve.tensor_scalar(nblk[:], bank[7][:, E:2 * E], float(P - 1), None, ALU.add))
            link(dve.tensor_copy(cnt_i[:], nblk[:]))
            link(dve.tensor_scalar(cnt_i[:], cnt_i[:], P.bit_length() - 1, None, ALU.logical_shift_right))
            link(dve.tensor_copy(nblk[:], cnt_i[:]))
            link(dve.tensor_tensor_scan(blocks_to[:], nblk[:], zeros_e[:], 0.0, ALU.add, ALU.add))
            link(dve.tensor_tensor(first_slot, blocks_to[:], nblk[:], ALU.subtract))
            link(dve.scalar_tensor_tensor(out=first_slot, in0=first_slot, scalar=float(P), in1=bank[7][:, 0:E],
                                          op0=ALU.mult, op1=ALU.add))
            link(dve.scalar_tensor_tensor(out=first_slot, in0=row_ends[:, 0:E], scalar=1.0, in1=first_slot,
                                          op0=ALU.add, op1=ALU.subtract))
            link(dve.tensor_tensor(diagonal, blocks_to[0:E, :], ident[0:E, 0:E], ALU.mult))
            link(dve.tensor_reduce(blocks_col, diagonal, AX_X, ALU.add))
            dve.tensor_scalar(past[:], iota_blk[0:E, :], blocks_col, None, ALU.is_ge).then_inc(past_ready, 1)
            link(dve.tensor_tensor(rest, running, over_t(first_slot), ALU.subtract))
            for k, hit in enumerate((hit0, hit1)):
                link(dve.tensor_tensor(product, hit, rest, ALU.mult))
                link(dve.tensor_reduce(slot[:, k * T:(k + 1) * T], by_tile(product), AX_X, ALU.add))
            link(dve.tensor_copy(slot_i[:], slot))
            dve.tensor_scalar(part_i[:, 0, :], slot_i[:], P - 1, None, ALU.bitwise_and)
            link(dve.tensor_scalar(part_i[:, 1, :], slot_i[:], P.bit_length() - 1, None, ALU.logical_shift_right))
            link(dve.tensor_copy(part_b[:], part_i[:]))
            dve.wait_ge(expert_counted, 1)
            link(dve.tensor_scalar(exp_f[:], bank[7][:, 2 * E:2 * E + BLOCKS], float(E - 1), None, ALU.min))
            dve.tensor_copy(used_blocks[:], blocks_to[:, E - 1:E])
            dve.tensor_copy(expert_of[:], exp_f[:]).then_inc(expert_of_ready, 1)

            def group(a, h, n):
                cols = a[:, bass.ds(h.value(G), G)]
                return cols.rearrange("p (o g) -> p o g", o=1).to_broadcast([P, n, G])

            def hots(h):
                u = h.c % 2
                if has(h - 2, HOTS):
                    wait_tiles(dve, hot_used, h, plus=-1)
                dve.tensor_tensor(blk_hot[:, u, 0, :, :], iota_rep[:, 0:BLOCKS, :], group(part_b[:, 1, :], h, BLOCKS),
                                  ALU.is_equal).then_inc(equal_ready, 1)
                dve.tensor_tensor(lo_hot[:, u, :, :], iota_rep[:], group(part_b[:, 0, :], h, P), ALU.is_equal)
                wait_tiles(dve, equal_ready, h, plus=1)
                dve.tensor_tensor(blk_hot[:, u, 2, :, :], blk_hot[:, u, 0, :, :], group(choice_no, h, BLOCKS),
                                  ALU.mult).then_inc(hot_ready, 1)

            pipeline(dve, 2, HOTS - 1, HOTS - 1, hots)

            dve.wait_ge(hot_used, HOTS)
            link(dve.tensor_copy(code_f[:], bank[6][:, BLOCKS:2 * BLOCKS]))
            link(dve.scalar_tensor_tensor(out=dest_f[:], in0=bank[6][:, 0:BLOCKS], scalar=float(K * T), in1=code_f[:],
                                          op0=ALU.mult, op1=ALU.add))
            link(dve.tensor_scalar(row_f[:], dest_f[:], -1.0, 0.0, ALU.add, ALU.max))
            link(dve.tensor_copy(dest_g[:], row_f[:]))
            dve.tensor_scalar(token_of[:], dest_g[:], 1, None, ALU.logical_shift_right).then_inc(tables_ready, 1)
            link(dve.tensor_scalar(empty_f[:], code_f[:], 0.0, float(NO_ROW), ALU.is_equal, ALU.mult))
            link(dve.scalar_tensor_tensor(out=row_f[:], in0=dest_f[:], scalar=-1.0, in1=empty_f[:], op0=ALU.add, op1=ALU.add))
            link(dve.tensor_copy(dest_of[:], row_f[:]))
            dve.wait_ge(egap_ready, 1)
            link(dve.tensor_scalar(m0, egap, 1.0, None, ALU.add))
            link(dve.reciprocal(gate[:, 0, :], m0))
            link(dve.tensor_tensor(gate[:, 1, :], egap, gate[:, 0, :], ALU.mult))
            dve.wait_ge(expert_of_ready, 1)
            dve.wait_ge(consts_loaded, 64)

            def keep(t):
                wait_tiles(dve, z_in_turned, t, plus=1)
                if has(t - 2, BLOCKS):
                    wait_tiles(dve, hidden_done, t, plus=-1)
                dve.tensor_copy(zT_in[:, t.c % 2, :], bank[t.c % 2][:, 0:C]).then_inc(zT_in_ready, 1)

            def add_b2(t):
                u = t.c % RING
                if has(t - RING, BLOCKS):
                    wait_filled(dve, moe_stored, t, used=1)
                dve.tensor_copy(s_idx[:, u, :], col(dest_of, t)).then_inc(s_idx_ready, 1)
                e = expert(dve, t)
                wait_tiles(dve, expert_done, t, plus=1)
                dve.tensor_tensor(moe_out[:, u, :], bank[4 + t.c % 2][:, 0:C],
                                  b2_all[:, bass.ds(e, 1), :].rearrange("p o c -> p (o c)"), ALU.add).then_inc(moe_ready, 1)

            used = blocks_used(dve)

            def experts(t):
                for stage, of in ((keep, t), (add_b2, t - 2)):
                    if has(of, BLOCKS):
                        with if_used(dve, used, of):
                            stage(of)

            pipeline(dve, 6, FULL_BLOCKS - 1, BLOCKS + 1, experts)

            def output(t):
                a, m, n, g = t, t - 1, t - 2, t - 5
                if has(a):
                    wait_apart(dve, (y_done, a, 1))
                    dve.bn_stats(bn_y[:, a.c % 2, :], bank[a.c % 8][:, 0:C]).then_inc(y_bn, 1)
                if has(m):
                    wait_apart(dve, (y_bn, m, 1))
                    dve.bn_aggr(y_mv_buf[:, m.c % RING, :], bn_y[:, m.c % 2, :]).then_inc(y_mv, 1)
                if has(a):
                    wait_tiles(dve, z_own_ready, a, plus=1)
                    dve.tensor_tensor(row(x2_all, a), row(x2_all, a), beta_all[:], ALU.add).then_inc(beta_added, 1)
                if has(m):
                    wait_tiles(dve, y_mv, m, plus=1)
                    if has(m - 2):
                        wait_tiles(dve, y_rs_ready, m, plus=-1)
                    dve.tensor_scalar(y_ve_buf[:, m.c % 2, :], y_mv_buf[:, m.c % RING, 1:2], EPS, None, ALU.add).then_inc(y_ve, 1)
                if has(g):
                    wait_tiles(dve, yn_ready, g, plus=1)
                    if has(g - 2):
                        wait_tiles(dve, res_ready, g, plus=-1)
                    dve.tensor_tensor(yg[:, g.c % 2, :], yn[:, g.c % RING, :], gamma_all[:], ALU.mult).then_inc(yg_ready, 1)
                if has(n):
                    wait_tiles(dve, y_rs_ready, n, plus=1)
                    if has(n - RING):
                        wait_tiles(dve, yn_ready, n, plus=1 - RING)
                    dve.tensor_scalar(nb_y[:, n.c % RING, :], y_mv_buf[:, n.c % RING, 0:1], y_rs[:, n.c % RING, :], -1.0, ALU.mult,
                                      ALU.mult).then_inc(nb_y_ready, 1)

            pipeline(dve, 8, T - 1, T + 4, output)


_INS = ["x", "dst_src", "L0_gnn_weight", "L0_gnn_attn_l", "L0_gnn_attn_r", "L0_ffn_gate_w", "L0_ffn_gate_b", "L0_ffn_w1",
        "L0_ffn_b1", "L0_ffn_w2", "L0_ffn_b2", "L0_ffn_gamma", "L0_ffn_beta"]


def kernel(**inputs):
    import numpy as _np
    import concourse.bacc as _bacc
    from concourse import mybir as _mybir
    from concourse.bass_utils import run_bass_kernel_spmd as _run

    given = dict(inputs)
    given["x"] = _np.concatenate([_np.asarray(inputs["x"]), _np.zeros((NP - N, C), _np.float32)])
    edges = _np.zeros((P, TG, 2), _np.int32)
    for at, name in ((0, "dst"), (1, "src")):
        whole = _np.zeros(NP, _np.int32)
        whole[:N] = _np.asarray(inputs[name])[:N]
        edges[:, :T, at] = whole.reshape(P, T)
    given["dst_src"] = edges

    nc = _bacc.Bacc("TRN2", target_bir_lowering=False, num_devices=1)
    arrays, args = {}, []
    for name in _INS:
        a = _np.ascontiguousarray(given[name])
        arrays[f"in_{name}_dram"] = a
        args.append(nc.dram_tensor(f"in_{name}_dram", a.shape, _mybir.dt.from_np(a.dtype), kind="ExternalInput").ap())
    args.append(nc.dram_tensor("out_0_dram", (NP, C), F32, kind="ExternalOutput").ap())
    bass_gnn_moe(nc, *args)
    r = _run(nc, [arrays], core_ids=[0])
    return r.results[0]["out_0_dram"][:N]
```
